# Optimizing a Trainium2 kernel written in Bass

```python
import numpy as np
import jax
import jax.numpy as jnp

def _softmax(x, axis=-1):
    return jax.nn.softmax(x, axis=axis)

def _gelu(x):
    return jax.nn.gelu(x, approximate=True)

def _silu(x):
    return jax.nn.silu(x)

def _sigmoid(x):
    return jax.nn.sigmoid(x)

def _layernorm(x, axis=-1, eps=1e-05):
    m = jnp.mean(x, axis=axis, keepdims=True)
    v = jnp.var(x, axis=axis, keepdims=True)
    return (x - m) / jnp.sqrt(v + eps)

def _scatter_add(tgt, idx, src, axis=0):
    return tgt.at[idx].add(src)

def _segment_sum(src, seg, n):
    return jax.ops.segment_sum(src, seg, n)
kernel_name = 'mk_seq_postln_d1_jaxref_r8_9f4dc8'

def setup_inputs(seed: int=0):
    np.random.seed(seed)
    _w = jnp.asarray

    def _L0_attn_setup():
        import jax, jax.numpy as jnp
        import numpy as np
        HID = 128
        NH = 4
        HD = HID // NH
        KS = 4
        C = 64
        EPS = 1e-05
        B = 4
        L = 512

        def _causal_dwconv(x, w):
            xc = jnp.moveaxis(x, 1, 2)
            y = jax.lax.conv_general_dilated(xc, w, window_strides=(1,), padding=[(w.shape[-1] - 1, 0)], dimension_numbers=('NCH', 'OIH', 'NCH'), feature_group_count=w.shape[0])
            return jnp.moveaxis(jax.nn.silu(y), 1, 2)

        def _forward(x, Wq, Wk, Wv, Wb, conv_q, conv_k, conv_v, g, Wo):
            Bx, Lx, _ = x.shape
            N = Lx // C
            q = _causal_dwconv(x @ Wq, conv_q).reshape(Bx, Lx, NH, HD)
            k = _causal_dwconv(x @ Wk, conv_k).reshape(Bx, Lx, NH, HD)
            v = _causal_dwconv(x @ Wv, conv_v).reshape(Bx, Lx, NH, HD)
            q = q / jnp.linalg.norm(q, axis=-1, keepdims=True)
            k = k / jnp.linalg.norm(k, axis=-1, keepdims=True)
            beta = jax.nn.sigmoid(x @ Wb)
            Q = q.reshape(Bx, N, C, NH, HD)
            K = k.reshape(Bx, N, C, NH, HD)
            V = v.reshape(Bx, N, C, NH, HD)
            bta = beta.reshape(Bx, N, C, NH, 1)
            Kb = K * bta
            Vb = V * bta
            A = jnp.einsum('bnihd,bnjhd->bnij', Kb, K)
            T0 = jnp.eye(C, dtype=x.dtype) - jnp.tril(A, -1)
            col = jnp.arange(C)

            def body(i, T):
                row = jax.lax.dynamic_slice_in_dim(T, i, 1, axis=2)[:, :, 0]
                acc = jnp.einsum('bnj,bnjc->bnc', row, T)
                new_row = jnp.where(col < i, row + acc, row)
                return jax.lax.dynamic_update_slice_in_dim(T, new_row[:, :, None, :], i, axis=2)
            T = jax.lax.fori_loop(1, C, body, T0)
            W = jnp.einsum('bnij,bnjhd->bnihd', T, Kb)
            U = jnp.einsum('bnij,bnjhd->bnihd', T, Vb)

            def chunk_step(S, inp):
                q_i, k_i, w_i, u0 = inp
                Sd = jnp.diagonal(S, axis1=-2, axis2=-1)
                u_i = u0 - w_i * Sd[:, None]
                o_inter = q_i * Sd[:, None]
                A_i = jnp.tril(jnp.einsum('bchd,bchd->bc', q_i, k_i))
                o_intra = A_i[:, :, None, None] * u_i
                S = S + jnp.einsum('bchd,bche->bhde', k_i, u_i)
                return (S, o_inter + o_intra)
            xs = tuple((jnp.moveaxis(a, 1, 0) for a in (Q, K, W, U)))
            S0 = jnp.zeros((Bx, NH, HD, HD), x.dtype)
            S, O = jax.lax.scan(chunk_step, S0, xs)
            o = jnp.moveaxis(O, 0, 1).reshape(Bx, Lx, NH, HD)
            o = o * jax.lax.rsqrt(jnp.mean(o * o, axis=-1, keepdims=True) + EPS) * g
            out = o.reshape(Bx, Lx, NH * HD) @ Wo
            return (out, S)

        def _reference_tuple_inner(x, Wq, Wk, Wv, Wb, conv_q, conv_k, conv_v, g, Wo):
            return _forward(x, Wq, Wk, Wv, Wb, conv_q, conv_k, conv_v, g, Wo)
        key = jax.random.key(seed)
        ks = jax.random.split(key, 9)
        return {'x': jax.random.normal(ks[0], (B, L, HID), jnp.float32), 'Wq': jax.random.normal(ks[1], (HID, HID), jnp.float32) * 0.02, 'Wk': jax.random.normal(ks[2], (HID, HID), jnp.float32) * 0.02, 'Wv': jax.random.normal(ks[3], (HID, HID), jnp.float32) * 0.02, 'Wb': jax.random.normal(ks[4], (HID, NH), jnp.float32) * 0.02, 'conv_q': jax.random.normal(ks[5], (HID, 1, KS), jnp.float32) * 0.5, 'conv_k': jax.random.normal(ks[6], (HID, 1, KS), jnp.float32) * 0.5, 'conv_v': jax.random.normal(ks[7], (HID, 1, KS), jnp.float32) * 0.5, 'g': jnp.ones((HD,), jnp.float32), 'Wo': jax.random.normal(ks[8], (HID, HID), jnp.float32) * 0.02}
    _L0_attn_in = _L0_attn_setup()

    def _L0_ffn_setup():
        import jax, jax.numpy as jnp
        import numpy as np
        H = 128
        I = 88
        E = 64
        TOP_K = 8
        NG = 8
        TOPK_GROUP = 4
        N_SHARED = 2
        ROUTED_SCALE = 2.5
        S_I = I * N_SHARED

        def _route(x, gate_w, gate_bias):
            T = x.shape[0]
            logits = x @ gate_w.T
            scores = jax.nn.sigmoid(logits)
            scores_for_choice = scores + gate_bias[None, :]
            grp = scores_for_choice.reshape(T, NG, E // NG)
            group_scores = jnp.sum(jax.lax.top_k(grp, 2)[0], axis=-1)
            _, gidx = jax.lax.top_k(group_scores, TOPK_GROUP)
            gmask = jnp.zeros((T, NG), dtype=scores.dtype).at[jnp.arange(T)[:, None], gidx].set(1.0)
            emask = jnp.repeat(gmask, E // NG, axis=1)
            masked = jnp.where(emask > 0, scores_for_choice, 0.0)
            _, topk_idx = jax.lax.top_k(masked, TOP_K)
            topk_w = jnp.take_along_axis(scores, topk_idx, axis=1)
            topk_w = topk_w / (jnp.sum(topk_w, axis=-1, keepdims=True) + 1e-20)
            topk_w = topk_w * ROUTED_SCALE
            rw = jnp.zeros((T, E), dtype=scores.dtype).at[jnp.arange(T)[:, None], topk_idx].add(topk_w)
            return rw

        def _mlp(x, gw, uw, dw):
            return jax.nn.silu(x @ gw.T) * (x @ uw.T) @ dw.T
        key = jax.random.key(seed)
        ks = jax.random.split(key, 10)
        sc = 0.02
        return {'hidden_states': jax.random.normal(ks[0], (1, 128, H), dtype=jnp.float32), 'gate_w': sc * jax.random.normal(ks[1], (E, H), dtype=jnp.float32), 'gate_bias': sc * jax.random.normal(ks[2], (E,), dtype=jnp.float32), 'Wg': sc * jax.random.normal(ks[3], (E, I, H), dtype=jnp.float32), 'Wu': sc * jax.random.normal(ks[4], (E, I, H), dtype=jnp.float32), 'Wd': sc * jax.random.normal(ks[5], (E, H, I), dtype=jnp.float32), 'Sg': sc * jax.random.normal(ks[6], (S_I, H), dtype=jnp.float32), 'Su': sc * jax.random.normal(ks[7], (S_I, H), dtype=jnp.float32), 'Sd': sc * jax.random.normal(ks[8], (H, S_I), dtype=jnp.float32)}
    _L0_ffn_in = _L0_ffn_setup()
    _d = {'L0_attn_x': _L0_attn_in['x'], 'L0_attn_Wq': _L0_attn_in['Wq'], 'L0_attn_Wk': _L0_attn_in['Wk'], 'L0_attn_Wv': _L0_attn_in['Wv'], 'L0_attn_Wb': _L0_attn_in['Wb'], 'L0_attn_conv_q': _L0_attn_in['conv_q'], 'L0_attn_conv_k': _L0_attn_in['conv_k'], 'L0_attn_conv_v': _L0_attn_in['conv_v'], 'L0_attn_g': _L0_attn_in['g'], 'L0_attn_Wo': _L0_attn_in['Wo'], 'L0_ffn_gate_w': _L0_ffn_in['gate_w'], 'L0_ffn_gate_bias': _L0_ffn_in['gate_bias'], 'L0_ffn_Wg': _L0_ffn_in['Wg'], 'L0_ffn_Wu': _L0_ffn_in['Wu'], 'L0_ffn_Wd': _L0_ffn_in['Wd'], 'L0_ffn_Sg': _L0_ffn_in['Sg'], 'L0_ffn_Su': _L0_ffn_in['Su'], 'L0_ffn_Sd': _L0_ffn_in['Sd']}
    _x0 = _d['L0_attn_x']
    _d['L0_attn_x'] = jax.random.normal(jax.random.fold_in(jax.random.key(seed), 1), (8, 512, 128), dtype=_x0.dtype)
    del _x0
    return _d

def reference(L0_attn_x, L0_attn_Wq, L0_attn_Wk, L0_attn_Wv, L0_attn_Wb, L0_attn_conv_q, L0_attn_conv_k, L0_attn_conv_v, L0_attn_g, L0_attn_Wo, L0_ffn_gate_w, L0_ffn_gate_bias, L0_ffn_Wg, L0_ffn_Wu, L0_ffn_Wd, L0_ffn_Sg, L0_ffn_Su, L0_ffn_Sd):

    def _L0_attn_ref(x, Wq, Wk, Wv, Wb, conv_q, conv_k, conv_v, g, Wo):
        import jax, jax.numpy as jnp
        import numpy as np
        HID = 128
        NH = 4
        HD = HID // NH
        KS = 4
        C = 64
        EPS = 1e-05
        B = 4
        L = 512

        def _causal_dwconv(x, w):
            xc = jnp.moveaxis(x, 1, 2)
            y = jax.lax.conv_general_dilated(xc, w, window_strides=(1,), padding=[(w.shape[-1] - 1, 0)], dimension_numbers=('NCH', 'OIH', 'NCH'), feature_group_count=w.shape[0])
            return jnp.moveaxis(jax.nn.silu(y), 1, 2)

        def _forward(x, Wq, Wk, Wv, Wb, conv_q, conv_k, conv_v, g, Wo):
            Bx, Lx, _ = x.shape
            N = Lx // C
            q = _causal_dwconv(x @ Wq, conv_q).reshape(Bx, Lx, NH, HD)
            k = _causal_dwconv(x @ Wk, conv_k).reshape(Bx, Lx, NH, HD)
            v = _causal_dwconv(x @ Wv, conv_v).reshape(Bx, Lx, NH, HD)
            q = q / jnp.linalg.norm(q, axis=-1, keepdims=True)
            k = k / jnp.linalg.norm(k, axis=-1, keepdims=True)
            beta = jax.nn.sigmoid(x @ Wb)
            Q = q.reshape(Bx, N, C, NH, HD)
            K = k.reshape(Bx, N, C, NH, HD)
            V = v.reshape(Bx, N, C, NH, HD)
            bta = beta.reshape(Bx, N, C, NH, 1)
            Kb = K * bta
            Vb = V * bta
            A = jnp.einsum('bnihd,bnjhd->bnij', Kb, K)
            T0 = jnp.eye(C, dtype=x.dtype) - jnp.tril(A, -1)
            col = jnp.arange(C)

            def body(i, T):
                row = jax.lax.dynamic_slice_in_dim(T, i, 1, axis=2)[:, :, 0]
                acc = jnp.einsum('bnj,bnjc->bnc', row, T)
                new_row = jnp.where(col < i, row + acc, row)
                return jax.lax.dynamic_update_slice_in_dim(T, new_row[:, :, None, :], i, axis=2)
            T = jax.lax.fori_loop(1, C, body, T0)
            W = jnp.einsum('bnij,bnjhd->bnihd', T, Kb)
            U = jnp.einsum('bnij,bnjhd->bnihd', T, Vb)

            def chunk_step(S, inp):
                q_i, k_i, w_i, u0 = inp
                Sd = jnp.diagonal(S, axis1=-2, axis2=-1)
                u_i = u0 - w_i * Sd[:, None]
                o_inter = q_i * Sd[:, None]
                A_i = jnp.tril(jnp.einsum('bchd,bchd->bc', q_i, k_i))
                o_intra = A_i[:, :, None, None] * u_i
                S = S + jnp.einsum('bchd,bche->bhde', k_i, u_i)
                return (S, o_inter + o_intra)
            xs = tuple((jnp.moveaxis(a, 1, 0) for a in (Q, K, W, U)))
            S0 = jnp.zeros((Bx, NH, HD, HD), x.dtype)
            S, O = jax.lax.scan(chunk_step, S0, xs)
            o = jnp.moveaxis(O, 0, 1).reshape(Bx, Lx, NH, HD)
            o = o * jax.lax.rsqrt(jnp.mean(o * o, axis=-1, keepdims=True) + EPS) * g
            out = o.reshape(Bx, Lx, NH * HD) @ Wo
            return (out, S)

        def _reference_tuple_inner(x, Wq, Wk, Wv, Wb, conv_q, conv_k, conv_v, g, Wo):
            return _forward(x, Wq, Wk, Wv, Wb, conv_q, conv_k, conv_v, g, Wo)
        return _reference_tuple_inner(x, Wq, Wk, Wv, Wb, conv_q, conv_k, conv_v, g, Wo)[0]

    def _L0_ffn_ref(hidden_states, gate_w, gate_bias, Wg, Wu, Wd, Sg, Su, Sd):
        import jax, jax.numpy as jnp
        import numpy as np
        H = 128
        I = 88
        E = 64
        TOP_K = 8
        NG = 8
        TOPK_GROUP = 4
        N_SHARED = 2
        ROUTED_SCALE = 2.5
        S_I = I * N_SHARED

        def _route(x, gate_w, gate_bias):
            T = x.shape[0]
            logits = x @ gate_w.T
            scores = jax.nn.sigmoid(logits)
            scores_for_choice = scores + gate_bias[None, :]
            grp = scores_for_choice.reshape(T, NG, E // NG)
            group_scores = jnp.sum(jax.lax.top_k(grp, 2)[0], axis=-1)
            _, gidx = jax.lax.top_k(group_scores, TOPK_GROUP)
            gmask = jnp.zeros((T, NG), dtype=scores.dtype).at[jnp.arange(T)[:, None], gidx].set(1.0)
            emask = jnp.repeat(gmask, E // NG, axis=1)
            masked = jnp.where(emask > 0, scores_for_choice, 0.0)
            _, topk_idx = jax.lax.top_k(masked, TOP_K)
            topk_w = jnp.take_along_axis(scores, topk_idx, axis=1)
            topk_w = topk_w / (jnp.sum(topk_w, axis=-1, keepdims=True) + 1e-20)
            topk_w = topk_w * ROUTED_SCALE
            rw = jnp.zeros((T, E), dtype=scores.dtype).at[jnp.arange(T)[:, None], topk_idx].add(topk_w)
            return rw

        def _mlp(x, gw, uw, dw):
            return jax.nn.silu(x @ gw.T) * (x @ uw.T) @ dw.T
        B, S, _ = hidden_states.shape
        x = hidden_states.reshape(B * S, H)
        rw = _route(x, gate_w, gate_bias)
        expert_out = jax.vmap(lambda gw_, uw_, dw_: _mlp(x, gw_, uw_, dw_))(Wg, Wu, Wd)
        routed = jnp.einsum('eth,te->th', expert_out, rw)
        shared = _mlp(x, Sg, Su, Sd)
        out = (routed + shared).reshape(B, S, H)
        return out
    x = L0_attn_x
    x = _layernorm(x + _L0_attn_ref(x, L0_attn_Wq, L0_attn_Wk, L0_attn_Wv, L0_attn_Wb, L0_attn_conv_q, L0_attn_conv_k, L0_attn_conv_v, L0_attn_g, L0_attn_Wo), axis=-1)
    x = _layernorm(x + _L0_ffn_ref(x, L0_ffn_gate_w, L0_ffn_gate_bias, L0_ffn_Wg, L0_ffn_Wu, L0_ffn_Wd, L0_ffn_Sg, L0_ffn_Su, L0_ffn_Sd), axis=-1)
    return x

_drawn_inputs = setup_inputs


def setup_inputs(seed=0):
    import zlib

    import numpy as np

    out = dict(_drawn_inputs(seed))
    spreads = {'L0_attn_g': (1.0, 0.2)}
    factors = {'L0_ffn_gate_w': 8.0,
     'L0_ffn_gate_bias': 8.0,
     'L0_ffn_Wg': 8.0,
     'L0_ffn_Wu': 8.0,
     'L0_ffn_Wd': 8.0,
     'L0_ffn_Sg': 8.0,
     'L0_ffn_Su': 8.0,
     'L0_ffn_Sd': 8.0}
    for name, (base, spread) in spreads.items():
        noise = np.random.default_rng([zlib.crc32(name.encode()), seed]).standard_normal(out[name].shape)
        drawn = base * np.exp(spread * noise) if base else spread * noise
        out[name] = jnp.asarray(drawn.astype(out[name].dtype))
    for name, factor in factors.items():
        out[name] = (out[name] * factor).astype(out[name].dtype)
    return out
```

```python
from contextlib import ExitStack

import concourse.bass as bass
from concourse import mybir

F32 = mybir.dt.float32
F32R = mybir.dt.float32r
U32 = mybir.dt.uint32
ALU = mybir.AluOpType
ACT = mybir.ActivationFunctionType
AX = mybir.AxisListType

P = 128
B, L, D = 8, 512, 128
NH, HD = 4, 32
KS = 4
C = 64
NT = L // P
NC = L // C
LEVELS = 6
E, I, TOPK, NG, GROUPS_KEPT = 64, 88, 8, 8, 4
EG = E // NG
ER = 8
EP = P // ER
RG = E // EP
TPG = I // ER
NR = RG * TPG
NS = 2
NJ = NS + NR
SHARED = NS * I
HIDDEN = SHARED + NR * P
RING = 4
CHUNK = 512
NCHUNK = NR * P // CHUNK
LN_EPS, RMS_EPS = 1e-5, 1e-5
ROUTED_SCALE = 2.5
TAKEN = -3.0e38

QKV = 3 * D
QKVB = QKV + NH

C_ID, C_NEG, C_POS, C_ROWS, C_BEFORE, C_ONE = 0, 128, 130, 132, 140, 204
C_ALL = 205


def block_program(nc, x_tok, x_chan, Wq, Wk, Wv, Wb, conv_q, conv_k, conv_v, g_rms, Wo,
                  gate_wT, gate_bias, gateT, upT, downT, shared_gateT, shared_upT, shared_downT,
                  consts, masks, out):
    with ExitStack() as ctx:
        def sb(name, shape, dt=F32):
            return ctx.enter_context(nc.sbuf_tensor(name, shape, dt))

        def bank(name):
            return ctx.enter_context(nc.psum_tensor(name, [P, 512], F32))

        def sem(name):
            return ctx.enter_context(nc.semaphore(name))

        gate_hi, gate_lo = sb("gate_hi", [P, HIDDEN], F32R), sb("gate_lo", [P, HIDDEN], F32R)
        up_hi, up_lo = sb("up_hi", [P, HIDDEN], F32R), sb("up_lo", [P, HIDDEN], F32R)
        down_sh = sb("down_sh", [P, NS, 2, P], F32R)
        down_ring = sb("down_ring", [P, RING, 2, P], F32R)
        down_dram = nc.dram_tensor("down_pairs", [NR, P, 2, P], F32, kind="Internal").ap()
        tap_hi, tap_lo = sb("tap_hi", [P, KS, QKVB], F32R), sb("tap_lo", [P, KS, QKVB], F32R)
        router_hi, router_lo = sb("router_hi", [P, E], F32R), sb("router_lo", [P, E], F32R)
        wo_g = sb("wo_g", [P, D])
        const = sb("const", [P, C_ALL])
        mask = sb("mask", [P, 2 * LEVELS, P])
        bias_b = sb("bias_b", [P, E])
        g_col = sb("g_col", [P, 1])
        minus_half = sb("minus_half", [P, 32])

        xc_raw = sb("xc_raw", [P, L])
        xc_hi, xc_lo = sb("xc_hi", [P, L + KS], F32R), sb("xc_lo", [P, L + KS], F32R)
        x_res = sb("x_res", [P, NT, D])
        arena = sb("arena", [P, 13 * 512])

        def part(at, n):
            return arena[:, at * 512:(at + n) * 512]

        qkv = part(0, 3).rearrange("p (i c) -> p i c", i=NT)
        kb, vb = part(3, 1).rearrange("p (i c) -> p i c", i=NT), part(4, 1).rearrange("p (i c) -> p i c", i=NT)
        temp1, temp2 = part(5, 1).rearrange("p (i c) -> p i c", i=NT), part(6, 1).rearrange("p (i c) -> p i c", i=NT)
        squares = part(5, 2)
        k_chan, kb_chan = part(7, 1), part(8, 1)
        inv, inv_t = part(9, 1), part(10, 1)
        neg_a_t, z_sb = part(11, 1), part(12, 1)
        o_sb, on_sb = part(7, 1).rearrange("p (i c) -> p i c", i=NT), part(8, 1).rearrange("p (i c) -> p i c", i=NT)
        on_chan, r1 = part(11, 1), part(12, 1).rearrange("p (i c) -> p i c", i=NT)
        score, choice = arena[:, 0:256], arena[:, 256:512]
        masked, replaced = arena[:, 512:768], arena[:, 768:1024]
        tour1, tour2 = arena[:, 1024:1280], arena[:, 1280:1536]
        conv_b, w_raw = part(0, 3), arena[:, 1536:1536 + QKVB]
        tap_raw = arena[:, 2560:2560 + KS * QKVB].rearrange("p (k n) -> p k n", k=KS)
        small_raw = arena[:, 4608:4608 + 2 * SHARED + E + NS * P + D]

        tanh_b = sb("tanh_b", [P, NT, NH])
        beta = sb("beta", [P, NT, NH])
        head_ss, head_rn = sb("head_ss", [P, NT * 2 * NH]), sb("head_rn", [P, NT * 2 * NH])
        decay, state = sb("decay", [P, NC]), sb("state", [P, NC + 1])
        qk_dot = sb("qk_dot", [P, NT])
        rms_ss, rms_r = sb("rms_ss", [P, NT * NH]), sb("rms_r", [P, NT * NH])
        stats, mean_var, rstd = sb("stats", [P, NT, 6]), sb("mean_var", [P, NT, 2]), sb("rstd", [P, NT])
        var_eps = sb("var_eps", [P, NT])
        stats2, mean_var2, rstd2 = sb("stats2", [P, NT, 6]), sb("mean_var2", [P, NT, 2]), sb("rstd2", [P, NT])
        var_eps2 = sb("var_eps2", [P, NT])
        x1 = [sb(f"x1_{n}", [P, NT, D]) for n in range(2)]
        x1_hi = [sb(f"x1_hi{n}", [P, L], F32R) for n in range(2)]
        x1_lo = [sb(f"x1_lo{n}", [P, L], F32R) for n in range(2)]
        group_sum, group_rank, group_on = sb("group_sum", [P, 32]), sb("group_rank", [P, 32]), sb("group_on", [P, 32])
        top8 = sb("top8", [P, NT, 8])
        weight_sum, weight_inv = sb("weight_sum", [P, NT]), sb("weight_inv", [P, NT])
        routing = sb("routing", [P, NT, E])
        route_rows = sb("route_rows", [P, RG, L])
        expert_rows = sb("expert_rows", [E, L])
        work = sb("work", [P, 6, L])
        act_g, prod, hid = work[:, 0:2, :], work[:, 2:4, :], work[:, 4:6, :]
        hid_hi = sb("hid_hi", [P, 2, L], F32R)
        hid_lo = sb("hid_lo", [P, 2, L], F32R)
        y_chan = sb("y_chan", [P, L])
        r2 = sb("r2", [P, NT, D])

        gate_ps = [bank(f"gate_ps{n}") for n in range(2)]
        up_ps = [bank(f"up_ps{n}") for n in range(2)]
        y_ps = bank("y_ps")
        pa, pb, pc = bank("pa"), bank("pb"), bank("pc")

        ident = const[:, C_ID:C_ID + P]

        names = """consts_in small_in conv_in chunk_in0 chunk_in1 chunk_in2 chunk_in3 chunk_in4 chunk_in5
            half_set zero_set tap_made wo_made small_hi small_lo taps_hi taps_lo
            chunk_hi chunk_lo down_out0 down_out1 shared_in
            x_in0 x_in1 xhi_done xlo_done qkv_mm qkv_act sq_done beta_done ss_done rn_done qk_done vb_done kb_done
            kt_mm kt_done kbt_mm kbt_done eye_set a_mm at_mm nat_done inv0_done invt0_done
            z_mm z_done inv_done invt_done
            xk_mm g_done p1_done p2_done ab_mm decay_done state_done sdb_mm ksd_done osd_done y_done
            tr_mm u_done dot_done dotr_done dotw_done uw_done o_done osq_done orms_done orr_done on_done
            ont_mm ont_done wo_mm r1_done st_done mv_done ve_done rstd_done x1_done x1t_mm x1hi_done x1lo_done
            logit_mm tanh_done score_done choice_done t_done gs_done gt_done rank_done gon_done mask_done
            masked_done top_done rep_done w_done ws_done wi_done rw_done route_mm route_done
            gate_mm up_mm s_done m_done h_done hhi_done hlo_done down_mm
            ring0 ring1 ring2 ring3 route_in0 route_in1 route_in2 route_in3 sx_done
            yc_done yt_mm r2_done st2_done mv2_done ve2_done rstd2_done ln2_done out_done0""".split()
        s = {n: sem(n) for n in names}

        class Sems:
            pass
        S = type("S", (), s)
        ring_in = [S.ring0, S.ring1, S.ring2, S.ring3]
        chunk_in = [[S.chunk_in0, S.chunk_in1], [S.chunk_in2, S.chunk_in3], [S.chunk_in4, S.chunk_in5]]
        down_out = [S.down_out0, S.down_out1]
        inv_mm = [None] + [sem(f"inv_mm{k}") for k in range(1, LEVELS)]
        invt_mm = [None] + [sem(f"invt_mm{k}") for k in range(1, LEVELS - 1)]
        route_in = [S.route_in0, S.route_in1, S.route_in2, S.route_in3]

        def cols(j):
            return (j * I, (j + 1) * I) if j < NS else (SHARED + (j - NS) * P, SHARED + (j - NS + 1) * P)

        def rows(j):
            return I if j < NS else P

        def blk(ap, i):
            return ap[:, i * P:(i + 1) * P]

        def mask_of(level, transposed):
            return mask[:, 2 * level + transposed, :].bitcast(U32).unsqueeze(1).broadcast_to([P, NT, P])

        def as_tiles(ap):
            return ap.rearrange("p (i c) -> p i c", i=NT)

        def past(n):
            return n + 1

        block = ctx.enter_context(nc.Block())

        @block.sync
        def _(sp):
            def load_x(b):
                sp.wait_ge(S.xlo_done, past(b))
                sp.wait_ge(S.r1_done, past(b))
                sp.dma_start(xc_raw[:, :], x_chan[:, bass.ds(b * L, L)]).then_inc(S.x_in0, 16)
                sp.dma_start(x_res[:, :, :], x_tok[bass.ds(b, 1), :, :].rearrange("o (i p) c -> p (o i) c", p=P)).then_inc(S.x_in1, 16)

            def load_chunk(c, n):
                for m, src in enumerate((gateT, upT, downT)):
                    sp.dma_start(work[:, 2 * m + n, :], src[:, bass.ds(c * CHUNK, CHUNK)]).then_inc(chunk_in[m][n], 16)

            def load_down(b, j):
                n = (j - NS) % RING
                if j - NS >= RING:
                    sp.wait_ge(S.down_mm, past(b * NJ + j - RING + 1))
                else:
                    sp.wait_ge(S.down_mm, past(b * NJ))
                sp.dma_start(down_ring[:, n, :, :].bitcast(F32), down_dram[j - NS]).then_inc(ring_in[n], 16)

            sp.dma_start(const[:, :], consts).then_inc(S.consts_in, 16)
            for n, w in enumerate((conv_q, conv_k, conv_v)):
                sp.dma_start(conv_b[:, n * 512:(n + 1) * 512],
                             w.rearrange("c o k -> o (c k)").broadcast_to([P, D * KS])).then_inc(S.conv_in, 16)
            for n, w in enumerate((Wq, Wk, Wv)):
                sp.dma_start(w_raw[:, n * D:(n + 1) * D], w).then_inc(S.conv_in, 16)
            sp.dma_start(w_raw[:, QKV:QKVB], Wb).then_inc(S.conv_in, 16)
            sp.dma_start(mask[:, :, :], masks).then_inc(S.small_in, 16)
            sp.dma_start(small_raw[:, 0:SHARED], shared_gateT).then_inc(S.small_in, 16)
            sp.dma_start(small_raw[:, SHARED:2 * SHARED], shared_upT).then_inc(S.small_in, 16)
            sp.dma_start(small_raw[:, 2 * SHARED:2 * SHARED + E], gate_wT).then_inc(S.small_in, 16)
            sp.dma_start(small_raw[0:I, 2 * SHARED + E:2 * SHARED + E + NS * P], shared_downT).then_inc(S.small_in, 16)
            sp.dma_start(small_raw[:, 2 * SHARED + E + NS * P:2 * SHARED + E + NS * P + D], Wo).then_inc(S.small_in, 16)
            sp.dma_start(bias_b[:, :], gate_bias.rearrange("(o e) -> o e", o=1).broadcast_to([P, E])).then_inc(S.small_in, 16)
            for h in range(NH):
                sp.dma_start(g_col[h * HD:(h + 1) * HD, :], g_rms.rearrange("(d o) -> d o", o=1)).then_inc(S.small_in, 16)
            load_chunk(0, 0)
            load_chunk(1, 1)
            with sp.Fori(1, NCHUNK // 2) as c2:
                for n in range(2):
                    sp.wait_ge(S.chunk_lo, 3 * (2 * c2 + n - 1))
                    load_chunk(2 * c2 + n, n)
            sp.wait_ge(S.chunk_lo, 3 * (NCHUNK - 2))
            load_chunk(NCHUNK - 1, 0)
            for n in range(2):
                sp.wait_ge(down_out[n], 16 * ((NCHUNK + 1 - n) // 2))
            with sp.Fori(0, B) as b:
                load_x(b)
                for j in range(NS, NJ):
                    load_down(b, j)
            sp.wait_ge(S.out_done0, past(16 * B))

        @block.gpsimd
        def _(pool):
            def attention(b, step):
                if step == 8:
                    pool.wait_ge(S.beta_done, b + 1)
                    pool.tensor_tensor(vb.rearrange("p i (h d) -> p i h d", h=NH),
                                       qkv[:, :, 2 * D:].rearrange("p i (h d) -> p i h d", h=NH),
                                       beta[:, :, :].unsqueeze(3).broadcast_to([P, NT, NH, HD]),
                                       ALU.mult).then_inc(S.vb_done, 1)
                if 9 <= step < 9 + NT:
                    i = step - 9
                    pool.wait_ge(S.ss_done, b + 1)
                    pool.tensor_tensor(head_rn[:, 8 * i:8 * i + 8], head_ss[:, 8 * i:8 * i + 8],
                                       minus_half[:, 0:8], ALU.pow).then_inc(S.rn_done, 1)
                if step == 14:
                    pool.wait_ge(S.qk_done, b + 1)
                    pool.tensor_tensor(kb.rearrange("p i (h d) -> p i h d", h=NH),
                                       qkv[:, :, D:2 * D].rearrange("p i (h d) -> p i h d", h=NH),
                                       beta[:, :, :].unsqueeze(3).broadcast_to([P, NT, NH, HD]),
                                       ALU.mult).then_inc(S.kb_done, 1)
                if step == 15:
                    eye = ident.unsqueeze(1).broadcast_to([P, NT, P])
                    pool.tensor_copy(as_tiles(inv), eye)
                    pool.tensor_copy(as_tiles(inv_t), eye).then_inc(S.eye_set, 1)
                if step == 18:
                    pool.tensor_tensor(temp1, qkv[:, :, 0:D], qkv[:, :, D:2 * D], ALU.mult).then_inc(S.dot_done, 1)
                if step == 31:
                    pool.wait_ge(S.g_done, b + 1)
                    pool.tensor_tensor(as_tiles(neg_a_t), as_tiles(z_sb), kb, ALU.mult).then_inc(S.p1_done, 1)
                if step == 34:
                    pool.wait_ge(S.ksd_done, b + 1)
                    pool.tensor_tensor(temp1, vb, temp2, ALU.subtract).then_inc(S.y_done, 1)
                if step == 36:
                    pool.wait_ge(S.u_done, b + 1)
                    pool.wait_ge(S.dotw_done, b + 1)
                    pool.tensor_tensor(temp2, temp2, qk_dot[:, :].unsqueeze(2).broadcast_to([P, NT, D]),
                                       ALU.mult).then_inc(S.uw_done, 1)
                if step == 39:
                    pool.wait_ge(S.orms_done, b + 1)
                    pool.tensor_tensor(rms_r[:, :], rms_ss[:, :], minus_half[:, 0:NT * NH], ALU.pow).then_inc(S.orr_done, 1)
                if step == 43:
                    pool.wait_ge(S.ve_done, b + 1)
                    pool.tensor_tensor(rstd[:, :], var_eps[:, :], minus_half[:, 0:NT], ALU.pow).then_inc(S.rstd_done, 1)

            def weighted(b, j):
                if j < NS:
                    w = const[0:I, C_ONE:C_ONE + 1].broadcast_to([I, L])
                else:
                    pool.wait_ge(route_in[(j - NS) // TPG], 16 * (b + 1))
                    w = route_rows[:, (j - NS) // TPG, :]
                pool.wait_ge(S.m_done, past(b * NJ + j + 1))
                pool.wait_ge(S.hlo_done, past(b * NJ + max(0, j - 1)))
                m = rows(j)
                pool.tensor_tensor(hid[0:m, j % 2, :], prod[0:m, j % 2, :], w, ALU.mult).then_inc(S.h_done, 1)

            def ln2(b):
                pool.wait_ge(S.ve2_done, b + 1)
                pool.tensor_tensor(rstd2[:, :], var_eps2[:, :], minus_half[:, 0:NT], ALU.pow).then_inc(S.rstd2_done, 1)

            pool.sem_inc(S.h_done, 1)
            pool.memset(minus_half[:, :], -0.5).then_inc(S.half_set, 1)
            pool.wait_ge(S.half_set, 1)
            pool.wait_ge(S.consts_in, 16)

            def store_down(c, n):
                pool.wait_ge(S.half_set, 1)
                pool.wait_ge(S.chunk_lo, 3 * (c + 1))
                pool.dma_start(down_dram[bass.ds(c * (CHUNK // P), CHUNK // P)].rearrange("t p h c -> p t h c"),
                               route_rows[:, 2 * n:2 * n + 2, :].rearrange("p u (t h c) -> p (u t) h c", h=2, c=P)
                               ).then_inc(down_out[n], 16)
            with pool.Fori(0, NCHUNK // 2) as c2:
                for n in range(2):
                    store_down(2 * c2 + n, n)
            store_down(NCHUNK - 1, 0)
            with pool.Fori(0, B) as b:
                for step in range(NJ):
                    attention(b, step)
                for j in range(NJ):
                    weighted(b, j)
                ln2(b)

        @block.scalar
        def _(act):
            def attention(b, step):
                if step == 0:
                    act.wait_ge(S.x_in0, 16 * (b + 1))
                    act.wait_ge(S.qkv_mm, past(NT * b))
                    act.activation(xc_hi[:, KS:KS + L], xc_raw[:, :], ACT.Copy).then_inc(S.xhi_done, 1)
                if 3 <= step < 3 + NT:
                    i = step - 3
                    ps = (pa, pb)[i % 2]
                    act.wait_ge(S.qkv_mm, past(NT * b + i + 1))
                    act.wait_ge(S.rw_done, past(b))
                    act.activation(qkv[:, i, :], ps[:, 0:QKV], ACT.Silu)
                    act.activation(tanh_b[:, i, :], ps[:, QKV:QKVB], ACT.Tanh, scale=0.5).then_inc(S.qkv_act, 1)
                if step == 7:
                    act.wait_ge(S.qkv_act, NT * (b + 1))
                    act.activation(squares.rearrange("p (i c) -> p i c", i=NT), qkv[:, :, 0:2 * D],
                                   ACT.Square).then_inc(S.sq_done, 1)
                if step == 15:
                    act.wait_ge(S.kt_mm, b + 1)
                    act.activation(k_chan, pa[:, :], ACT.Copy).then_inc(S.kt_done, 1)
                if step == 16:
                    act.wait_ge(S.kbt_mm, b + 1)
                    act.activation(kb_chan, pb[:, :], ACT.Copy, scale=-1.0).then_inc(S.kbt_done, 1)
                if step == 18:
                    act.wait_ge(S.at_mm, b + 1)
                    act.activation(neg_a_t, pa[:, :], ACT.Copy).then_inc(S.nat_done, 1)
                for k in range(1, LEVELS):
                    if step == 18 + 2 * k:
                        act.wait_ge(S.z_mm, (LEVELS - 1) * b + k)
                        act.activation(z_sb, pb[:, :], ACT.Copy).then_inc(S.z_done, 1)
                if step == 37:
                    act.wait_ge(S.o_done, b + 1)
                    act.activation(temp1, o_sb, ACT.Square).then_inc(S.osq_done, 1)
                if step == 41:
                    act.wait_ge(S.ont_mm, b + 1)
                    act.activation(on_chan, pc[:, :], ACT.Copy).then_inc(S.ont_done, 1)
                if step == 44:
                    act.wait_ge(S.x1t_mm, b + 1)
                    act.activation(x1_hi[0][:, :], pb[:, :], ACT.Copy).then_inc(S.x1hi_done, 1)

            def router(b):
                act.wait_ge(S.logit_mm, b + 1)
                act.activation(score, pc[:, 0:NT * E], ACT.Tanh, scale=0.5).then_inc(S.tanh_done, 1)
                act.wait_ge(S.route_mm, b + 1)
                act.activation(expert_rows[:, :], pa[0:E, :], ACT.Copy).then_inc(S.route_done, 1)
                act.wait_ge(S.route_done, past(b + 1))
                act.wait_ge(S.h_done, past(NJ * b))
                for g in range(RG):
                    act.dma_start(route_rows[:, g, :], expert_rows[g * EP:(g + 1) * EP, :].unsqueeze(1)
                                  .broadcast_to([EP, ER, L])).then_inc(route_in[g], 16)

            def silu_tile(b, j):
                m = rows(j)
                act.wait_ge(S.gate_mm, b * NJ + j + 1)
                act.wait_ge(S.m_done, past(b * NJ + max(0, j - 1)))
                act.activation(act_g[0:m, j % 2, :], gate_ps[j % 2][0:m, :], ACT.Silu).then_inc(S.s_done, 1)

            def hidden_hi(b, j):
                m = rows(j)
                act.wait_ge(S.h_done, past(b * NJ + j + 1))
                act.wait_ge(S.down_mm, past(b * NJ + max(0, j - 1)))
                act.activation(hid_hi[0:m, j % 2, :], hid[0:m, j % 2, :], ACT.Copy).then_inc(S.hhi_done, 1)

            for start in (S.s_done, S.route_done, S.out_done0):
                act.sem_inc(start, 1)
            act.wait_ge(S.tap_made, 1)
            act.activation(tap_hi[:, :, :], tap_raw, ACT.Copy).then_inc(S.taps_hi, 1)
            act.wait_ge(S.small_in, 16 * 11)
            act.activation(gate_hi[:, 0:SHARED], small_raw[:, 0:SHARED], ACT.Copy)
            act.activation(up_hi[:, 0:SHARED], small_raw[:, SHARED:2 * SHARED], ACT.Copy)
            act.activation(router_hi[:, :], small_raw[:, 2 * SHARED:2 * SHARED + E], ACT.Copy)
            act.activation(down_sh[0:I, :, 0, :], small_raw[0:I, 2 * SHARED + E:2 * SHARED + E + NS * P]
                           .rearrange("p (s c) -> p s c", s=NS), ACT.Copy).then_inc(S.small_hi, 1)

            def chunk_high(c, n):
                at = SHARED + c * CHUNK
                for m, hi in enumerate((gate_hi, up_hi)):
                    act.wait_ge(chunk_in[m][n], 16 * ((c - n) // 2 + 1) if isinstance(c, int) else 16 * (c_pair[0] + 1))
                    act.activation(hi[:, bass.ds(at, CHUNK)], work[:, 2 * m + n, :], ACT.Copy).then_inc(S.chunk_hi, 1)
                act.wait_ge(chunk_in[2][n], 16 * ((c - n) // 2 + 1) if isinstance(c, int) else 16 * (c_pair[0] + 1))
                act.activation(pairs(n)[:, :, 0, :], work[:, 4 + n, :].rearrange("p (t c) -> p t c", c=P),
                               ACT.Copy).then_inc(S.chunk_hi, 1)

            def pairs(n):
                return route_rows[:, 2 * n:2 * n + 2, :].rearrange("p u (t h c) -> p (u t) h c", h=2, c=P).bitcast(F32R)

            c_pair = [None]
            chunk_high(0, 0)
            chunk_high(1, 1)
            with act.Fori(1, NCHUNK // 2) as c2:
                c_pair[0] = c2
                for n in range(2):
                    act.wait_ge(down_out[n], 16 * c2)
                    chunk_high(2 * c2 + n, n)
            act.wait_ge(down_out[0], 16 * (NCHUNK // 2))
            chunk_high(NCHUNK - 1, 0)

            with act.Fori(0, B) as b:
                for step in range(NJ):
                    attention(b, step)
                router(b)
                for j in range(NJ + 1):
                    if j < NJ:
                        silu_tile(b, j)
                    if j >= 1:
                        hidden_hi(b, j - 1)
                act.wait_ge(S.down_mm, past(NJ * (b + 1)))
                act.activation(y_chan[:, :], y_ps[:, :], ACT.Copy).then_inc(S.yc_done, 1)
                act.wait_ge(S.ln2_done, b + 1)
                act.dma_start(out[bass.ds(b, 1), :, :].rearrange("o (i p) c -> p (o i) c", p=P),
                              r2[:, :, :]).then_inc(S.out_done0, 16)

        @block.vector
        def _(dve):
            def attention(b, step):
                if step == 1:
                    dve.wait_ge(S.xhi_done, b + 1)
                    dve.tensor_tensor(xc_lo[:, KS:KS + L], xc_raw[:, :], xc_hi[:, KS:KS + L].bitcast(F32),
                                      ALU.subtract).then_inc(S.xlo_done, 1)
                if step == 7:
                    dve.wait_ge(S.qkv_act, NT * (b + 1))
                    dve.tensor_scalar(beta[:, :, :], tanh_b[:, :, :], 0.5, 0.5, ALU.mult, ALU.add).then_inc(S.beta_done, 1)
                if step == 8:
                    dve.wait_ge(S.sq_done, b + 1)
                    dve.tensor_reduce(head_ss[:, :], squares.rearrange("p (g d) -> p g d", d=HD), AX.X,
                                      ALU.add).then_inc(S.ss_done, 1)
                if step == 13:
                    dve.wait_ge(S.rn_done, NT * (b + 1))
                    qk = qkv[:, :, 0:2 * D].rearrange("p i (g d) -> p i g d", d=HD)
                    dve.tensor_tensor(qk, qk, head_rn[:, :].rearrange("p (i g) -> p i g", i=NT).unsqueeze(3)
                                      .broadcast_to([P, NT, 2 * NH, HD]), ALU.mult).then_inc(S.qk_done, 1)
                if step == 18:
                    dve.wait_ge(S.zero_set, 1)
                    dve.wait_ge(S.a_mm, b + 1)
                    dve.wait_ge(S.eye_set, b + 1)
                    dve.copy_predicated(as_tiles(inv), mask_of(0, 0), as_tiles(pc[:, :])).then_inc(S.inv_done, 1)
                if step == 19:
                    dve.wait_ge(S.zero_set, 1)
                    dve.wait_ge(S.nat_done, b + 1)
                    dve.copy_predicated(as_tiles(inv_t), mask_of(0, 1), as_tiles(neg_a_t)).then_inc(S.invt_done, 1)
                if step == 20:
                    dve.wait_ge(S.dot_done, b + 1)
                    dve.tensor_reduce(qk_dot[:, :], temp1, AX.X, ALU.add).then_inc(S.dotr_done, 1)
                    dve.wait_ge(S.dotr_done, b + 1)
                    dve.tensor_tensor(qk_dot[:, :], qk_dot[:, :], const[:, bass.ds(b + C_ROWS, 1)].broadcast_to([P, NT]),
                                      ALU.mult).then_inc(S.dotw_done, 1)
                for k in range(1, LEVELS):
                    if step == 19 + 2 * k:
                        dve.wait_ge(S.zero_set, 1)
                        dve.wait_ge(inv_mm[k], b + 1)
                        dve.copy_predicated(as_tiles(inv), mask_of(k, 0), as_tiles(pc[:, :])).then_inc(S.inv_done, 1)
                        if k < LEVELS - 1:
                            dve.wait_ge(S.zero_set, 1)
                            dve.wait_ge(invt_mm[k], b + 1)
                            dve.copy_predicated(as_tiles(inv_t), mask_of(k, 1), as_tiles(pa[:, :])).then_inc(S.invt_done, 1)
                if step == 30:
                    dve.wait_ge(S.xk_mm, b + 1)
                    dve.scalar_tensor_tensor(out=as_tiles(z_sb), in0=as_tiles(pb[:, :]), scalar=1.5,
                                             in1=qkv[:, :, D:2 * D], op0=ALU.mult, op1=ALU.subtract).then_inc(S.g_done, 1)
                if step == 31:
                    dve.wait_ge(S.g_done, b + 1)
                    dve.tensor_tensor(temp2, as_tiles(z_sb), vb, ALU.mult).then_inc(S.p2_done, 1)
                if step == 32:
                    dve.wait_ge(S.ab_mm, b + 1)
                    dve.tensor_scalar(decay[:, :], pc[:, 0:NC], 1.0, None, ALU.add).then_inc(S.decay_done, 1)
                    dve.wait_ge(S.decay_done, b + 1)
                    dve.tensor_tensor_scan(state[:, 1:NC + 1], decay[:, :], pc[:, NC:2 * NC], 0.0,
                                           ALU.mult, ALU.add).then_inc(S.state_done, 1)
                    dve.wait_ge(S.state_done, b + 1)
                    dve.tensor_copy(z_sb.rearrange("p (n c) -> p n c", c=C),
                                    state[:, 0:NC].unsqueeze(2).broadcast_to([P, NC, C])).then_inc(S.sx_done, 1)
                if step == 33:
                    dve.wait_ge(S.sdb_mm, b + 1)
                    dve.tensor_tensor(temp2, kb, as_tiles(pa[:, :]), ALU.mult).then_inc(S.ksd_done, 1)
                    dve.tensor_tensor(o_sb, qkv[:, :, 0:D], as_tiles(pa[:, :]), ALU.mult).then_inc(S.osd_done, 1)
                if step == 35:
                    dve.wait_ge(S.tr_mm, b + 1)
                    dve.scalar_tensor_tensor(out=temp2, in0=as_tiles(pb[:, :]), scalar=1.5,
                                             in1=temp1, op0=ALU.mult, op1=ALU.subtract).then_inc(S.u_done, 1)
                if step == 36:
                    dve.wait_ge(S.uw_done, b + 1)
                    dve.wait_ge(S.osd_done, b + 1)
                    dve.tensor_tensor(o_sb, o_sb, temp2, ALU.add).then_inc(S.o_done, 1)
                if step == 38:
                    dve.wait_ge(S.osq_done, b + 1)
                    dve.tensor_reduce(rms_ss[:, :], temp1.rearrange("p i (h d) -> p (i h) d", d=HD), AX.X,
                                      ALU.add).then_inc(S.t_done, 1)
                    dve.wait_ge(S.t_done, b + 1)
                    dve.tensor_scalar(rms_ss[:, :], rms_ss[:, :], 1.0 / HD, RMS_EPS, ALU.mult,
                                      ALU.add).then_inc(S.orms_done, 1)
                if step == 40:
                    dve.wait_ge(S.orr_done, b + 1)
                    dve.tensor_tensor(on_sb.rearrange("p i (h d) -> p i h d", h=NH),
                                      o_sb.rearrange("p i (h d) -> p i h d", h=NH),
                                      rms_r[:, :].rearrange("p (i h) -> p i h", i=NT).unsqueeze(3)
                                      .broadcast_to([P, NT, NH, HD]), ALU.mult).then_inc(S.on_done, 1)
                if step == 42:
                    dve.wait_ge(S.wo_mm, b + 1)
                    dve.wait_ge(S.x_in1, 16 * (b + 1))
                    dve.tensor_tensor(r1, as_tiles(pa[:, :]), x_res[:, :, :], ALU.add).then_inc(S.r1_done, 1)
                    moments(b, r1, stats, mean_var, var_eps, S.r1_done,  S.st_done, S.mv_done, S.ve_done)
                if step == 43:
                    dve.wait_ge(S.rstd_done, b + 1)
                    normalized(x1[0], r1, mean_var, rstd, S.x1_done)
                if step == 45:
                    dve.wait_ge(S.x1hi_done, b + 1)
                    dve.tensor_tensor(x1_lo[0][:, :], pb[:, :], x1_hi[0][:, :].bitcast(F32),
                                      ALU.subtract).then_inc(S.x1lo_done, 1)

            def moments(b, r, st, mv, ve, ready, st_sem, mv_sem, ve_sem):
                dve.wait_ge(ready, past(b + 1))
                for i in range(NT):
                    ins = dve.bn_stats(st[:, i, :], r[:, i, :])
                ins.then_inc(st_sem, 1)
                dve.wait_ge(S.zero_set, 1)
                dve.wait_ge(st_sem, b + 1)
                for i in range(NT):
                    ins = dve.bn_aggr(mv[:, i, :], st[:, i, :])
                ins.then_inc(mv_sem, 1)
                dve.wait_ge(mv_sem, b + 1)
                dve.tensor_scalar(ve[:, :], mv[:, :, 1], LN_EPS, None, ALU.add).then_inc(ve_sem, 1)

            def normalized(dst, r, mv, rs, done):
                for i in range(NT):
                    ins = dve.tensor_scalar(dst[:, i, :], r[:, i, :], mv[:, i, 0:1], rs[:, i:i + 1],
                                            ALU.subtract, ALU.mult)
                ins.then_inc(done, 1)

            def router(b):
                dve.wait_ge(S.tanh_done, b + 1)
                dve.tensor_scalar(score, score, 0.5, 0.5, ALU.mult, ALU.add).then_inc(S.score_done, 1)
                dve.wait_ge(S.score_done, b + 1)
                dve.tensor_tensor(choice.rearrange("p (i e) -> p i e", i=NT), score.rearrange("p (i e) -> p i e", i=NT),
                                  bias_b[:, :].unsqueeze(1).broadcast_to([P, NT, E]), ALU.add).then_inc(S.choice_done, 1)
                dve.wait_ge(S.choice_done, b + 1)
                c8 = choice.rearrange("p (g e) -> p g e", e=EG)
                hi4, lo4 = tour1[:, 0:128].rearrange("p (g e) -> p g e", e=4), tour1[:, 128:256].rearrange("p (g e) -> p g e", e=4)
                dve.tensor_tensor(hi4, c8[:, :, 0:4], c8[:, :, 4:8], ALU.max)
                dve.tensor_tensor(lo4, c8[:, :, 0:4], c8[:, :, 4:8], ALU.min).then_inc(S.gs_done, 1)
                dve.wait_ge(S.gs_done, 6 * b + 1)
                hi2, mid2 = tour2[:, 0:64].rearrange("p (g e) -> p g e", e=2), tour2[:, 64:128].rearrange("p (g e) -> p g e", e=2)
                lo2 = tour2[:, 128:192].rearrange("p (g e) -> p g e", e=2)
                dve.tensor_tensor(hi2, hi4[:, :, 0:2], hi4[:, :, 2:4], ALU.max)
                dve.tensor_tensor(mid2, hi4[:, :, 0:2], hi4[:, :, 2:4], ALU.min)
                dve.tensor_tensor(lo2, lo4[:, :, 0:2], lo4[:, :, 2:4], ALU.max).then_inc(S.gs_done, 1)
                dve.wait_ge(S.gs_done, 6 * b + 2)
                dve.tensor_tensor(lo2, lo2, mid2, ALU.max).then_inc(S.gs_done, 1)
                dve.wait_ge(S.gs_done, 6 * b + 3)
                hi1, mid1, lo1 = (tour1[:, n:n + 32].unsqueeze(2) for n in (0, 32, 64))
                dve.tensor_tensor(hi1, hi2[:, :, 0:1], hi2[:, :, 1:2], ALU.max)
                dve.tensor_tensor(mid1, hi2[:, :, 0:1], hi2[:, :, 1:2], ALU.min)
                dve.tensor_tensor(lo1, lo2[:, :, 0:1], lo2[:, :, 1:2], ALU.max).then_inc(S.gs_done, 1)
                dve.wait_ge(S.gs_done, 6 * b + 4)
                dve.tensor_tensor(lo1, lo1, mid1, ALU.max).then_inc(S.gs_done, 1)
                dve.wait_ge(S.gs_done, 6 * b + 5)
                dve.tensor_tensor(group_sum[:, :].unsqueeze(2), hi1, lo1, ALU.add).then_inc(S.gs_done, 1)
                dve.wait_ge(S.gs_done, 6 * b + 6)
                gs = group_sum[:, :].rearrange("p (i g) -> p i g", i=NT)
                other, own = gs.unsqueeze(2).broadcast_to([P, NT, NG, NG]), gs.unsqueeze(3).broadcast_to([P, NT, NG, NG])
                larger = tour1.rearrange("p (i g k) -> p i g k", i=NT, g=NG)
                equal = tour2.rearrange("p (i g k) -> p i g k", i=NT, g=NG)
                dve.tensor_tensor(larger, other, own, ALU.is_gt)
                dve.tensor_tensor(equal, other, own, ALU.is_equal).then_inc(S.gt_done, 1)
                dve.wait_ge(S.gt_done, 3 * b + 1)
                before = const[:, C_BEFORE:C_BEFORE + NG * NG].unsqueeze(1).broadcast_to([P, NT, NG * NG])
                dve.tensor_tensor(tour2.rearrange("p (i k) -> p i k", i=NT), tour2.rearrange("p (i k) -> p i k", i=NT),
                                  before, ALU.mult).then_inc(S.gt_done, 1)
                dve.wait_ge(S.gt_done, 3 * b + 2)
                dve.tensor_tensor(tour1, tour1, tour2, ALU.add).then_inc(S.gt_done, 1)
                dve.wait_ge(S.gt_done, 3 * b + 3)
                dve.tensor_reduce(group_rank[:, :], tour1.rearrange("p (g k) -> p g k", k=NG), AX.X, ALU.add).then_inc(S.rank_done, 1)
                dve.wait_ge(S.rank_done, b + 1)
                dve.tensor_scalar(group_on[:, :], group_rank[:, :], GROUPS_KEPT - 0.5, None, ALU.is_lt).then_inc(S.gon_done, 1)
                dve.wait_ge(S.gon_done, b + 1)
                dve.tensor_tensor(masked.rearrange("p (g e) -> p g e", e=EG), c8,
                                  group_on[:, :].unsqueeze(2).broadcast_to([P, NT * NG, EG]), ALU.mult).then_inc(S.mask_done, 1)
                dve.wait_ge(S.mask_done, b + 1)
                dve.tensor_scalar(masked, masked, 0.0, None, ALU.add).then_inc(S.masked_done, 1)
                dve.wait_ge(S.zero_set, 1)
                dve.wait_ge(S.masked_done, b + 1)
                for i in range(NT):
                    ins = dve.max(top8[:, i, :], masked[:, i * E:(i + 1) * E])
                ins.then_inc(S.top_done, 1)
                dve.wait_ge(S.zero_set, 1)
                dve.wait_ge(S.top_done, b + 1)
                for i in range(NT):
                    ins = dve.match_replace(replaced[:, i * E:(i + 1) * E], top8[:, i, :], masked[:, i * E:(i + 1) * E], TAKEN)
                ins.then_inc(S.rep_done, 1)
                dve.wait_ge(S.rep_done, b + 1)
                dve.scalar_tensor_tensor(out=tour1, in0=replaced, scalar=TAKEN, in1=score, op0=ALU.is_equal,
                                         op1=ALU.mult).then_inc(S.w_done, 1)
                dve.wait_ge(S.w_done, b + 1)
                dve.tensor_reduce(weight_sum[:, :], tour1.rearrange("p (i e) -> p i e", i=NT), AX.X, ALU.add).then_inc(S.ws_done, 1)
                dve.wait_ge(S.ws_done, 2 * b + 1)
                dve.tensor_scalar(weight_sum[:, :], weight_sum[:, :], 1e-20, None, ALU.add).then_inc(S.ws_done, 1)
                dve.wait_ge(S.ws_done, 2 * b + 2)
                dve.reciprocal(weight_inv[:, :], weight_sum[:, :]).then_inc(S.wi_done, 1)
                dve.wait_ge(S.wi_done, b + 1)
                dve.scalar_tensor_tensor(out=routing[:, :, :], in0=tour1.rearrange("p (i e) -> p i e", i=NT),
                                         scalar=ROUTED_SCALE, in1=weight_inv[:, :].unsqueeze(2).broadcast_to([P, NT, E]),
                                         op0=ALU.mult, op1=ALU.mult).then_inc(S.rw_done, 1)

            def product_tile(b, j):
                m = rows(j)
                dve.wait_ge(S.s_done, past(b * NJ + j + 1))
                dve.wait_ge(S.up_mm, b * NJ + j + 1)
                dve.wait_ge(S.h_done, past(b * NJ + max(0, j - 1)))
                dve.tensor_tensor(prod[0:m, j % 2, :], up_ps[j % 2][0:m, :], act_g[0:m, j % 2, :],
                                  ALU.mult).then_inc(S.m_done, 1)

            def hidden_lo(b, j):
                m = rows(j)
                dve.wait_ge(S.hhi_done, b * NJ + j + 1)
                dve.wait_ge(S.down_mm, past(b * NJ + max(0, j - 1)))
                dve.tensor_tensor(hid_lo[0:m, j % 2, :], hid[0:m, j % 2, :], hid_hi[0:m, j % 2, :].bitcast(F32),
                                  ALU.subtract).then_inc(S.hlo_done, 1)

            for start in (S.xlo_done, S.r1_done, S.m_done, S.hlo_done, S.rw_done, S.r2_done):
                dve.sem_inc(start, 1)
            dve.memset(xc_hi[:, 0:KS].bitcast(F32), 0.0)
            dve.memset(xc_lo[:, 0:KS].bitcast(F32), 0.0)
            dve.memset(state[:, 0:1], 0.0).then_inc(S.zero_set, 1)
            dve.wait_ge(S.conv_in, 16 * 7)
            for k in range(KS):
                dve.tensor_tensor(tap_raw[:, k, 0:QKV], w_raw[:, 0:QKV],
                                  conv_b.rearrange("p (n k) -> p n k", k=KS)[:, :, k], ALU.mult)
                ins = dve.tensor_copy(tap_raw[:, k, QKV:QKVB], w_raw[:, QKV:QKVB])
            ins.then_inc(S.tap_made, 1)
            dve.wait_ge(S.small_in, 16 * 11)
            at = 2 * SHARED + E + NS * P
            dve.tensor_scalar(wo_g[:, :], small_raw[:, at:at + D], g_col[:, 0:1], None, ALU.mult).then_inc(S.wo_made, 1)
            dve.wait_ge(S.taps_hi, 1)
            dve.tensor_tensor(tap_lo[:, :, :], tap_raw, tap_hi[:, :, :].bitcast(F32), ALU.subtract).then_inc(S.taps_lo, 1)
            dve.wait_ge(S.small_hi, 1)
            dve.tensor_tensor(gate_lo[:, 0:SHARED], small_raw[:, 0:SHARED], gate_hi[:, 0:SHARED].bitcast(F32), ALU.subtract)
            dve.tensor_tensor(up_lo[:, 0:SHARED], small_raw[:, SHARED:2 * SHARED], up_hi[:, 0:SHARED].bitcast(F32), ALU.subtract)
            dve.tensor_tensor(router_lo[:, :], small_raw[:, 2 * SHARED:2 * SHARED + E], router_hi[:, :].bitcast(F32), ALU.subtract)
            dve.tensor_tensor(down_sh[0:I, :, 1, :], small_raw[0:I, 2 * SHARED + E:at].rearrange("p (s c) -> p s c", s=NS),
                              down_sh[0:I, :, 0, :].bitcast(F32), ALU.subtract).then_inc(S.small_lo, 1)

            def chunk_low(c, n):
                at = SHARED + c * CHUNK
                for m, (hi, lo) in enumerate(((gate_hi, gate_lo), (up_hi, up_lo))):
                    dve.wait_ge(S.chunk_hi, 3 * c + m + 1)
                    dve.tensor_tensor(lo[:, bass.ds(at, CHUNK)], work[:, 2 * m + n, :],
                                      hi[:, bass.ds(at, CHUNK)].bitcast(F32), ALU.subtract).then_inc(S.chunk_lo, 1)
                dve.wait_ge(S.chunk_hi, 3 * c + 3)
                pair = route_rows[:, 2 * n:2 * n + 2, :].rearrange("p u (t h c) -> p (u t) h c", h=2, c=P)
                dve.tensor_tensor(pair[:, :, 1, :].bitcast(F32R), work[:, 4 + n, :].rearrange("p (t c) -> p t c", c=P),
                                  pair[:, :, 0, :], ALU.subtract).then_inc(S.chunk_lo, 1)

            with dve.Fori(0, NCHUNK // 2) as c2:
                for n in range(2):
                    chunk_low(2 * c2 + n, n)
            chunk_low(NCHUNK - 1, 0)

            with dve.Fori(0, B) as b:
                for step in range(NJ):
                    attention(b, step)
                router(b)
                for j in range(NJ + 1):
                    if j < NJ:
                        product_tile(b, j)
                    if j >= 1:
                        hidden_lo(b, j - 1)
                dve.wait_ge(S.yt_mm, b + 1)
                dve.wait_ge(S.out_done0, past(16 * b))
                dve.tensor_tensor(r2[:, :, :], as_tiles(y_ps[:, :]), x1[0][:, :, :], ALU.add).then_inc(S.r2_done, 1)
                moments(b, r2, stats2, mean_var2, var_eps2, S.r2_done, S.st2_done, S.mv2_done, S.ve2_done)
                dve.wait_ge(S.rstd2_done, b + 1)
                normalized(r2, r2, mean_var2, rstd2, S.ln2_done)

        @block.tensor
        def _(pe):
            def three(ps, lhs, rhs, start=True, stop=True):
                pe.matmul(ps, lhs[0], rhs[0], start=start, stop=False)
                pe.matmul(ps, lhs[0], rhs[1], start=False, stop=False)
                return pe.matmul(ps, lhs[1], rhs[0], start=False, stop=stop)

            def tiles(ps, lhs, rhs):
                for i in range(NT):
                    mm = pe.matmul(blk(ps, i), lhs(i), rhs(i), start=True, stop=True)
                return mm

            def turned(ps, src):
                for i in range(NT):
                    mm = pe.transpose(blk(ps, i), src(i), ident)
                return mm

            def attention(b, step):
                if 2 <= step < 2 + NT:
                    i = step - 2
                    ps = (pa, pb)[i % 2]
                    pe.wait_ge(S.xlo_done, past(b + 1))
                    if i < 2:
                        pe.wait_ge(S.route_done, past(b))
                    else:
                        pe.wait_ge(S.qkv_act, NT * b + i - 1)
                    for k in reversed(range(KS)):
                        n = QKVB if k == KS - 1 else QKV
                        at = i * P + k + 1
                        mm = three(ps[:, 0:n], (xc_hi[:, at:at + P], xc_lo[:, at:at + P]),
                                   (tap_hi[:, k, 0:n], tap_lo[:, k, 0:n]), start=(k == KS - 1), stop=(k == 0))
                    mm.then_inc(S.qkv_mm, 1)
                if step == 14:
                    pe.wait_ge(S.qk_done, b + 1)
                    turned(pa, lambda i: qkv[:, i, D:2 * D]).then_inc(S.kt_mm, 1)
                if step == 15:
                    pe.wait_ge(S.kb_done, b + 1)
                    turned(pb, lambda i: kb[:, i, :]).then_inc(S.kbt_mm, 1)
                if step == 17:
                    pe.wait_ge(S.kt_done, b + 1)
                    pe.wait_ge(S.kbt_done, b + 1)
                    tiles(pc, lambda i: blk(kb_chan, i), lambda i: blk(k_chan, i)).then_inc(S.a_mm, 1)
                    tiles(pa, lambda i: blk(k_chan, i), lambda i: blk(kb_chan, i)).then_inc(S.at_mm, 1)
                for k in range(1, LEVELS):
                    if step == 18 + 2 * k:
                        pe.wait_ge(S.nat_done, b + 1)
                        pe.wait_ge(S.inv_done, LEVELS * b + k)
                        tiles(pb, lambda i: blk(neg_a_t, i), lambda i: blk(inv, i)).then_inc(S.z_mm, 1)
                    if step == 19 + 2 * k:
                        pe.wait_ge(S.z_done, (LEVELS - 1) * b + k)
                        pe.wait_ge(S.invt_done, (LEVELS - 1) * b + k)
                        tiles(pc, lambda i: blk(inv_t, i), lambda i: blk(z_sb, i)).then_inc(inv_mm[k], 1)
                        if k < LEVELS - 1:
                            tiles(pa, lambda i: blk(z_sb, i), lambda i: blk(inv_t, i)).then_inc(invt_mm[k], 1)
                if step == 30:
                    pe.wait_ge(S.inv_done, LEVELS * (b + 1))
                    tiles(pb, lambda i: blk(inv, i), lambda i: qkv[:, i, D:2 * D]).then_inc(S.xk_mm, 1)
                if step == 32:
                    pe.wait_ge(S.p1_done, b + 1)
                    pe.wait_ge(S.p2_done, b + 1)
                    for i in range(NT):
                        pe.matmul(pc[:, 2 * i:2 * i + 2], blk(neg_a_t, i), const[:, C_NEG:C_NEG + 2], start=True, stop=True)
                    for i in range(NT):
                        mm = pe.matmul(pc[:, NC + 2 * i:NC + 2 * i + 2], temp2[:, i, :], const[:, C_POS:C_POS + 2],
                                       start=True, stop=True)
                    mm.then_inc(S.ab_mm, 1)
                if step == 33:
                    pe.wait_ge(S.sx_done, b + 1)
                    turned(pa, lambda i: blk(z_sb, i)).then_inc(S.sdb_mm, 1)
                if step == 35:
                    pe.wait_ge(S.y_done, b + 1)
                    tiles(pb, lambda i: blk(inv_t, i), lambda i: temp1[:, i, :]).then_inc(S.tr_mm, 1)
                if step == 40:
                    pe.wait_ge(S.on_done, b + 1)
                    turned(pc, lambda i: on_sb[:, i, :]).then_inc(S.ont_mm, 1)
                if step == 42:
                    pe.wait_ge(S.ont_done, b + 1)
                    tiles(pa, lambda i: blk(on_chan, i), lambda i: wo_g[:, :]).then_inc(S.wo_mm, 1)
                if step == 44:
                    pe.wait_ge(S.x1_done, b + 1)
                    turned(pb, lambda i: x1[0][:, i, :]).then_inc(S.x1t_mm, 1)

            def router(b):
                pe.wait_ge(S.x1lo_done, b + 1)
                for i in range(NT):
                    mm = three(pc[:, i * E:(i + 1) * E], (blk(x1_hi[0], i), blk(x1_lo[0], i)),
                               (router_hi[:, :], router_lo[:, :]))
                mm.then_inc(S.logit_mm, 1)
                pe.wait_ge(S.zero_set, 1)
                pe.wait_ge(S.rw_done, past(b + 1))
                for i in range(NT):
                    mm = pe.transpose(pa[0:E, i * P:(i + 1) * P], routing[:, i, :], ident)
                mm.then_inc(S.route_mm, 1)

            def gate_up(b, j):
                lo, hi = cols(j)
                m = rows(j)
                x = (x1_hi[0][:, :], x1_lo[0][:, :])
                pe.wait_ge(S.s_done, past(b * NJ + max(0, j - 1)))
                three(gate_ps[j % 2][0:m, :], (gate_hi[:, lo:hi], gate_lo[:, lo:hi]), x).then_inc(S.gate_mm, 1)
                pe.wait_ge(S.m_done, past(b * NJ + max(0, j - 1)))
                three(up_ps[j % 2][0:m, :], (up_hi[:, lo:hi], up_lo[:, lo:hi]), x).then_inc(S.up_mm, 1)

            def down(b, j):
                m = rows(j)
                if j >= NS:
                    n = (j - NS) % RING
                    pe.wait_ge(ring_in[n], 16 * (b * (NR // RING) + (j - NS) // RING + 1))
                    w = down_ring[:, n, 0, :], down_ring[:, n, 1, :]
                else:
                    w = down_sh[0:m, j, 0, :], down_sh[0:m, j, 1, :]
                pe.wait_ge(S.hlo_done, past(b * NJ + j + 1))
                if j == 0:
                    pe.wait_ge(S.r2_done, past(b))
                three(y_ps[:, :], w, (hid_hi[0:m, j % 2, :], hid_lo[0:m, j % 2, :]), start=(j == 0),
                      stop=(j == NJ - 1)).then_inc(S.down_mm, 1)

            for start in (S.down_mm, S.qkv_mm):
                pe.sem_inc(start, 1)
            pe.wait_ge(S.consts_in, 16)
            pe.wait_ge(S.zero_set, 1)
            pe.wait_ge(S.wo_made, 1)
            pe.wait_ge(S.taps_lo, 1)
            pe.wait_ge(S.small_lo, 1)
            pe.wait_ge(S.chunk_lo, 3 * NCHUNK)
            with pe.Fori(0, B) as b:
                for step in range(NJ):
                    attention(b, step)
                router(b)
                for j in range(NJ + 2):
                    if j < NJ:
                        gate_up(b, j)
                    if j >= 2:
                        down(b, j - 2)
                pe.wait_ge(S.yc_done, b + 1)
                turned(y_ps, lambda i: blk(y_chan, i)).then_inc(S.yt_mm, 1)


def kernel(**inputs):
    import numpy as np
    import concourse.bacc as bacc
    from concourse.bass_utils import run_bass_kernel_spmd

    def laid(name):
        return np.ascontiguousarray(inputs[name])

    x = laid("L0_attn_x")
    by_tile = lambda w: np.ascontiguousarray(
        w.reshape(RG, EP, TPG, ER, D).transpose(4, 0, 2, 1, 3).reshape(D, NR * P))
    wd = laid("L0_ffn_Wd").reshape(RG, EP, D, TPG, ER).transpose(1, 4, 0, 3, 2).reshape(P, NR * P)
    sd = laid("L0_ffn_Sd").T.reshape(NS, I, D).transpose(1, 0, 2).reshape(I, NS * D)

    consts = np.zeros((P, C_ALL), np.float32)
    t = np.arange(P)
    consts[:, C_ID:C_ID + P] = np.eye(P)
    consts[:, C_POS:C_POS + 2] = 2.0 * (t[:, None] // C == np.arange(2)[None, :])
    consts[:, C_NEG:C_NEG + 2] = -consts[:, C_POS:C_POS + 2]
    consts[:, C_ROWS:C_ROWS + B] = 2.0 * (t[:, None] % C <= np.arange(B)[None, :])
    consts[:, C_BEFORE:C_BEFORE + NG * NG] = np.tril(np.ones((NG, NG)), -1).reshape(1, -1)
    consts[:, C_ONE] = 1.0
    masks = np.zeros((P, 2 * LEVELS, P), np.float32)
    for k in range(LEVELS):
        n = 1 << k
        low = (t[:, None] // (2 * n) == t[None, :] // (2 * n)) & (t[:, None] // n % 2 == 1) & (t[None, :] // n % 2 == 0)
        masks[:, 2 * k] = low
        masks[:, 2 * k + 1] = low.T

    arrays = {
        "x_tok": x, "x_chan": np.ascontiguousarray(x.reshape(B * L, D).T),
        "Wq": laid("L0_attn_Wq"), "Wk": laid("L0_attn_Wk"), "Wv": laid("L0_attn_Wv"), "Wb": laid("L0_attn_Wb"),
        "conv_q": laid("L0_attn_conv_q"), "conv_k": laid("L0_attn_conv_k"), "conv_v": laid("L0_attn_conv_v"),
        "g_rms": laid("L0_attn_g"), "Wo": laid("L0_attn_Wo"),
        "gate_wT": np.ascontiguousarray(laid("L0_ffn_gate_w").T), "gate_bias": laid("L0_ffn_gate_bias"),
        "gateT": by_tile(laid("L0_ffn_Wg")), "upT": by_tile(laid("L0_ffn_Wu")), "downT": np.ascontiguousarray(wd),
        "shared_gateT": np.ascontiguousarray(laid("L0_ffn_Sg").T), "shared_upT": np.ascontiguousarray(laid("L0_ffn_Su").T),
        "shared_downT": np.ascontiguousarray(sd), "consts": consts, "masks": masks,
    }
    nc = bacc.Bacc("TRN2", target_bir_lowering=False, num_devices=1)
    args = [nc.dram_tensor(n, a.shape, mybir.dt.from_np(a.dtype), kind="ExternalInput").ap() for n, a in arrays.items()]
    args.append(nc.dram_tensor("out", (B, L, D), F32, kind="ExternalOutput").ap())
    block_program(nc, *args)
    r = run_bass_kernel_spmd(nc, [arrays], core_ids=[0])
    return r.results[0]["out"]
```

```python
from contextlib import ExitStack

import concourse.bass as bass
from concourse import mybir

F32 = mybir.dt.float32
F32R = mybir.dt.float32r
U32 = mybir.dt.uint32
ALU = mybir.AluOpType
ACT = mybir.ActivationFunctionType
AX = mybir.AxisListType

P = 128
B, L, D = 8, 512, 128
NH, HD = 4, 32
KS = 4
C = 64
NT = L // P
NC = L // C
LEVELS = 6
E, I, NG, GROUPS_KEPT = 64, 88, 8, 4
EG = E // NG
ER = 8
EP = P // ER
RG = E // EP
TPG = I // ER
NR = RG * TPG
NS = 2
NJ = NS + NR
SHARED = NS * I
HIDDEN = SHARED + NR * P
RING = 4
CHUNK = 512
NCHUNK = NR * P // CHUNK
LN_EPS, RMS_EPS = 1e-5, 1e-5
ROUTED_SCALE = 2.5
TAKEN = -3.0e38

HEAD = 8
MAIN = dict(turn_k=0, turn_kb=1, chunk_a=2, levels=3, turn_v=12, xk=13, products=14, sums=15, scan=16,
            spread=18, y=19, tr=21, o=21, osq=22, rms=23, on=26, turn_o=28, wo=30, moments=30, rstd=31, x1=31,
            x1_turn=34, x1_lo=34, logits=36, router=36, route=45, route_dma=45)
PRE = dict(x_load=10, x_hi=18, x_lo=20, conv=(22, 25, 32, 40), silu=(23, 27, 34, 41), sums=(25, 27, 34, 41),
           norms=(27, 28, 37, 43), norm=(29, 32, 38, 44), beta=42, vb=43)
FINISH = dict(y=3, moments=4, rstd=5, norm=5, store=6)
LAG = 3
HB = 4

QKV = 3 * D
QKVB = QKV + NH

C_ID, C_ROWS, C_BEFORE, C_ONE = 0, 128, 136, 200
C_ALL = 201


def block_program(nc, x_tok, x_chan, Wq, Wk, Wv, Wb, conv_q, conv_k, conv_v, g_rms, Wo,
                  gate_wT, gate_bias, gateT, upT, downT, shared_gateT, shared_upT, shared_downT,
                  consts, masks, out):
    with ExitStack() as ctx:
        def sb(name, shape, dt=F32):
            return ctx.enter_context(nc.sbuf_tensor(name, shape, dt))

        def bank(name):
            return ctx.enter_context(nc.psum_tensor(name, [P, 512], F32))

        def sem(name):
            return ctx.enter_context(nc.semaphore(name))

        gate_hi, gate_lo = sb("gate_hi", [P, HIDDEN], F32R), sb("gate_lo", [P, HIDDEN], F32R)
        up_hi, up_lo = sb("up_hi", [P, HIDDEN], F32R), sb("up_lo", [P, HIDDEN], F32R)
        down_sh = sb("down_sh", [P, NS, 2, P], F32R)
        down_ring = sb("down_ring", [P, RING, 2, P], F32R)
        down_dram = nc.dram_tensor("down_pairs", [NR, P, 2, P], F32, kind="Internal").ap()
        tap_hi, tap_lo = sb("tap_hi", [P, KS, QKVB], F32R), sb("tap_lo", [P, KS, QKVB], F32R)
        router_hi, router_lo = sb("router_hi", [P, E], F32R), sb("router_lo", [P, E], F32R)
        wo_g = sb("wo_g", [P, D])
        const = sb("const", [P, C_ALL])
        mask = sb("mask", [P, 2 * LEVELS, P])
        bias_b = sb("bias_b", [P, E])
        g_col = sb("g_col", [P, 1])
        minus_half = sb("minus_half", [P, 32])

        xc_raw = sb("xc_raw", [P, L])
        xc_hi, xc_lo = sb("xc_hi", [P, L + KS], F32R), sb("xc_lo", [P, L + KS], F32R)
        x_res = sb("x_res", [P, NT, D])
        arena = sb("arena", [P, 13 * 512])

        def part(at, n):
            return arena[:, at * 512:(at + n) * 512]

        qkv = part(0, 3).rearrange("p (i c) -> p i c", i=NT)
        kb, vb = part(3, 1).rearrange("p (i c) -> p i c", i=NT), part(4, 1).rearrange("p (i c) -> p i c", i=NT)
        temp1, temp2 = part(5, 1).rearrange("p (i c) -> p i c", i=NT), part(6, 1).rearrange("p (i c) -> p i c", i=NT)
        squares = part(5, 2)
        k_chan, kb_chan = part(7, 1), part(8, 1)
        inv, inv_t = part(9, 1), part(10, 1)
        neg_a_t, z_sb = part(11, 1), part(12, 1)
        vb_chan = part(11, 1)
        o_sb, on_sb = part(7, 1).rearrange("p (i c) -> p i c", i=NT), part(8, 1).rearrange("p (i c) -> p i c", i=NT)
        on_chan, r1 = part(11, 1), part(12, 1).rearrange("p (i c) -> p i c", i=NT)
        score, choice, masked, replaced, tour1, tour2 = (part(8, 3)[:, n * 256:(n + 1) * 256] for n in range(6))
        conv_b, w_raw = part(0, 3), arena[:, 1536:1536 + QKVB]
        tap_raw = arena[:, 2560:2560 + KS * QKVB].rearrange("p (k n) -> p k n", k=KS)
        small_raw = arena[:, 4608:4608 + 2 * SHARED + E + NS * P + D]

        tanh_b = sb("tanh_b", [P, NT, NH])
        beta = sb("beta", [P, NT, NH])
        head_ss, head_rn = sb("head_ss", [P, NT * 2 * NH]), sb("head_rn", [P, NT * 2 * NH])
        decay, state = sb("decay", [P, NC]), sb("state", [P, NC + 1])
        chunk_sums, addition = sb("chunk_sums", [P, 2 * NC]), sb("addition", [P, NC])
        qk_dot = sb("qk_dot", [P, NT])
        rms_ss, rms_r = sb("rms_ss", [P, NT * NH]), sb("rms_r", [P, NT * NH])
        stats, mean_var, rstd = sb("stats", [P, NT, 6]), sb("mean_var", [P, NT, 2]), sb("rstd", [P, NT])
        var_eps = sb("var_eps", [P, NT])
        stats2, mean_var2, rstd2 = sb("stats2", [P, NT, 6]), sb("mean_var2", [P, NT, 2]), sb("rstd2", [P, NT])
        var_eps2 = sb("var_eps2", [P, NT])
        x1 = [sb(f"x1_{n}", [P, NT, D]) for n in range(2)]
        x1_hi = [sb(f"x1_hi{n}", [P, L], F32R) for n in range(2)]
        x1_lo = [sb(f"x1_lo{n}", [P, L], F32R) for n in range(2)]
        group_sum, group_rank, group_on = sb("group_sum", [P, 32]), sb("group_rank", [P, 32]), sb("group_on", [P, 32])
        top8 = sb("top8", [P, NT, 8])
        weight_sum, weight_inv = sb("weight_sum", [P, NT]), sb("weight_inv", [P, NT])
        routing = sb("routing", [P, NT, E])
        route_rows = sb("route_rows", [P, RG, L])
        expert_rows = sb("expert_rows", [E, L])
        work = sb("work", [P, 6, L])
        act_g, prod, hid = work[:, 0:2, :], work[:, 2:4, :], work[:, 4:6, :]
        hid_hi = sb("hid_hi", [P, HB, L], F32R)
        hid_lo = sb("hid_lo", [P, HB, L], F32R)
        r2 = sb("r2", [P, NT, D])
        y_chan = r2[:, :, :].rearrange("p i c -> p (i c)")

        gate_ps = [bank(f"gate_ps{n}") for n in range(2)]
        up_ps = [bank(f"up_ps{n}") for n in range(2)]
        y_ps = bank("y_ps")
        pa, pb, pc = bank("pa"), bank("pb"), bank("pc")

        ident = const[:, C_ID:C_ID + P]
        eye = ident.unsqueeze(1).broadcast_to([P, NT, P])

        names = """eye_t_set vt_mm vt_done sums_done masks_in consts_in small_in conv_in chunk_in0 chunk_in1 chunk_in2
            chunk_in3 chunk_in4 chunk_in5 half_set zero_set tap_made wo_made small_hi small_lo
            taps_hi taps_lo chunk_hi chunk_lo down_out0 down_out1 x_in0 x_in1 xhi_done xlo_done
            qkv_mm qkv_act sq_done beta_done ss_done rn_done qk_done vb_done kb_done kt_mm kt_done
            kbt_mm kbt_done eye_set a_mm at_mm nat_done z_mm z_done inv_done invt_done xk_mm g_done
            p1_done p2_done decay_done state_done sdb_mm ksd_done osd_done y_done tr_mm u_done
            dot_done dotr_done dotw_done uw_done o_done osq_done orms_done orr_done on_done ont_mm
            ont_done wo_mm r1_done st_done mv_done ve_done rstd_done x1_done x1t_mm x1hi_done
            x1lo_done logit_mm tanh_done score_done choice_done t_done gs_done gt_done rank_done
            gon_done mask_done masked_done top_done rep_done w_done ws_done wi_done rw_done route_mm
            route_done gate_mm up_mm s_done m_done h_done hhi_done hlo_done down_mm ring0 ring1
            ring2 ring3 route_in0 route_in1 route_in2 route_in3 sx_done yc_done yt_mm r2_done
            st2_done mv2_done ve2_done rstd2_done ln2_done out_done0""".split()
        s = {n: sem(n) for n in names}

        S = type("S", (), s)
        ring_in = [S.ring0, S.ring1, S.ring2, S.ring3]
        chunk_in = [[S.chunk_in0, S.chunk_in1], [S.chunk_in2, S.chunk_in3], [S.chunk_in4, S.chunk_in5]]
        down_out = [S.down_out0, S.down_out1]
        inv_mm = [None] + [sem(f"inv_mm{k}") for k in range(1, LEVELS)]
        invt_mm = [None] + [sem(f"invt_mm{k}") for k in range(1, LEVELS - 1)]
        route_in = [S.route_in0, S.route_in1, S.route_in2, S.route_in3]

        def cols(j):
            return (j * I, (j + 1) * I) if j < NS else (SHARED + (j - NS) * P, SHARED + (j - NS + 1) * P)

        def rows(j):
            return I if j < NS else P

        def blk(ap, i):
            return ap[:, i * P:(i + 1) * P]

        def pairs(n):
            return route_rows[:, 2 * n:2 * n + 2, :].rearrange("p u (t h c) -> p (u t) h c", h=2, c=P)

        def mask_of(level, transposed):
            return mask[:, 2 * level + transposed, :].bitcast(U32).unsqueeze(1).broadcast_to([P, NT, P])

        def as_tiles(ap):
            return ap.rearrange("p (i c) -> p i c", i=NT)

        def place(j, n):
            return (n * NJ + j) % HB

        def some(n):
            return not isinstance(n, int) or n > 0

        def walk(engine, slot):
            for j in range(NJ):
                slot(j, -1, 1, False, True, True, False)
            for j in range(HEAD):
                slot(j, 0, 0, True, True, False, False)
            with engine.Fori(0, B - 3, 2) as b:
                for n in range(2):
                    at = [b + (n + m) for m in range(2)]
                    for m in range(1, 4):
                        engine.to_reg(b + (n + m))
                    for j in range(HEAD, NJ):
                        slot(j, at[0], n, True, True, True, False)
                    for j in range(HEAD):
                        slot(j, at[1], 1 - n, True, True, False, True)
            for j in range(HEAD, NJ):
                slot(j, B - 2, 0, True, True, False, False)
            for j in range(HEAD):
                slot(j, B - 1, 1, True, False, False, True)
            for j in range(HEAD, NJ):
                slot(j, B - 1, 1, True, False, False, False)
            for j in range(HEAD):
                slot(j, B, 0, False, False, False, True)

        block = ctx.enter_context(nc.Block())

        @block.sync
        def _(sp):
            def load_chunk(c):
                n = c % 2
                for m, src in enumerate((gateT, upT, downT)):
                    sp.dma_start(work[:, 2 * m + n, :], src[:, c * CHUNK:(c + 1) * CHUNK]).then_inc(chunk_in[m][n], 16)

            def store_down(c):
                n = c % 2
                sp.wait_ge(S.chunk_lo, 3 * (c + 1))
                sp.dma_start(down_dram[c * (CHUNK // P):(c + 1) * (CHUNK // P)].rearrange("t p h c -> p t h c"),
                             pairs(n)).then_inc(down_out[n], 16)

            def load_columns(c):
                if some(c):
                    sp.wait_ge(S.xlo_done, c)
                sp.dma_start(xc_raw[:, :], x_chan[:, bass.ds(c * L, L)]).then_inc(S.x_in0, 16)

            def load_residual(a):
                if some(a):
                    sp.wait_ge(S.r1_done, a)
                sp.dma_start(x_res[:, :, :], x_tok[bass.ds(a, 1), :, :].rearrange("o (i p) c -> p (o i) c", p=P)
                             ).then_inc(S.x_in1, 16)

            def load_route(a, g):
                used = (a - 1) * NJ + NS + (g + 1) * TPG
                if some(used):
                    sp.wait_ge(S.h_done, used)
                sp.wait_ge(S.route_done, a + 1)
                sp.dma_start(route_rows[:, g, :], expert_rows[g * EP:(g + 1) * EP, :].unsqueeze(1)
                             .broadcast_to([EP, ER, L])).then_inc(route_in[g], 16)

            def load_down(b, j):
                n = (j - NS) % RING
                used = b * NJ + (j - RING + 1 if j - NS >= RING else j - NS - RING + 1)
                if some(used):
                    sp.wait_ge(S.down_mm, used)
                sp.dma_start(down_ring[:, n, :, :].bitcast(F32), down_dram[j - NS]).then_inc(ring_in[n], 16)

            def slot(j, b, n, ffn, main, pre, finish):
                if main and not ffn and j % 3 == 0 and j // 3 < NCHUNK:
                    store_down(j // 3)
                    if j // 3 + 2 < NCHUNK:
                        load_chunk(j // 3 + 2)
                if main and not ffn and j == MAIN["route_dma"]:
                    for m in range(2):
                        sp.wait_ge(down_out[m], 16 * ((NCHUNK + 1 - m) // 2))
                if pre and j == PRE["x_load"]:
                    load_columns(b + 2)
                if main and j == MAIN["turn_k"]:
                    load_residual(b + 1)
                if main and j == MAIN["route_dma"]:
                    for g in range(RG - 1):
                        load_route(b + 1, g)
                if ffn and j == NS:
                    load_route(b, RG - 1)
                if ffn and j >= NS:
                    load_down(b, j)
                if finish and j == FINISH["store"]:
                    sp.wait_ge(S.ln2_done, b)
                    sp.dma_start(out[bass.ds(b - 1, 1), :, :].rearrange("o (i p) c -> p (o i) c", p=P),
                                 r2[:, :, :]).then_inc(S.out_done0, 16)

            for m, w in enumerate((conv_q, conv_k, conv_v)):
                sp.dma_start(conv_b[:, m * 512:(m + 1) * 512],
                             w.rearrange("c o k -> o (c k)").broadcast_to([P, D * KS])).then_inc(S.conv_in, 16)
            load_columns(0)
            at = 2 * SHARED + E
            sp.dma_start(small_raw[:, 0:SHARED], shared_gateT).then_inc(S.small_in, 16)
            sp.dma_start(small_raw[:, SHARED:2 * SHARED], shared_upT).then_inc(S.small_in, 16)
            sp.dma_start(small_raw[:, 2 * SHARED:at], gate_wT).then_inc(S.small_in, 16)
            sp.dma_start(small_raw[0:I, at:at + NS * P], shared_downT).then_inc(S.small_in, 16)
            sp.dma_start(small_raw[:, at + NS * P:at + NS * P + D], Wo).then_inc(S.small_in, 16)
            for h in range(NH):
                sp.dma_start(g_col[h * HD:(h + 1) * HD, :], g_rms.rearrange("(d o) -> d o", o=1)).then_inc(S.small_in, 16)
            load_chunk(0)
            load_chunk(1)
            sp.dma_start(mask[:, :, :], masks).then_inc(S.masks_in, 16)
            sp.dma_start(bias_b[:, :], gate_bias.rearrange("(o e) -> o e", o=1).broadcast_to([P, E])).then_inc(S.masks_in, 16)
            walk(sp, slot)
            sp.wait_ge(S.out_done0, 16 * B)

        @block.gpsimd
        def _(pool):
            def projections(c, j):
                for i in range(NT):
                    if j == PRE["norms"][i]:
                        pool.wait_ge(S.ss_done, NT * c + i + 1)
                        pool.tensor_tensor(head_rn[:, 8 * i:8 * i + 8], head_ss[:, 8 * i:8 * i + 8],
                                           minus_half[:, 0:8], ALU.pow).then_inc(S.rn_done, 1)
                if j == PRE["vb"]:
                    pool.wait_ge(S.beta_done, c + 1)
                    pool.tensor_tensor(vb.rearrange("p i (h d) -> p i h d", h=NH),
                                       qkv[:, :, 2 * D:].rearrange("p i (h d) -> p i h d", h=NH),
                                       beta[:, :, :].unsqueeze(3).broadcast_to([P, NT, NH, HD]),
                                       ALU.mult).then_inc(S.vb_done, 1)

            def attention(a, j):
                if j == MAIN["turn_k"]:
                    pool.wait_ge(S.qk_done, NT * (a + 1))
                    pool.tensor_tensor(kb.rearrange("p i (h d) -> p i h d", h=NH),
                                       qkv[:, :, D:2 * D].rearrange("p i (h d) -> p i h d", h=NH),
                                       beta[:, :, :].unsqueeze(3).broadcast_to([P, NT, NH, HD]),
                                       ALU.mult).then_inc(S.kb_done, 1)
                if j == MAIN["levels"]:
                    pool.tensor_tensor(temp1, qkv[:, :, 0:D], qkv[:, :, D:2 * D], ALU.mult).then_inc(S.dot_done, 1)
                if j == MAIN["products"]:
                    pool.wait_ge(S.g_done, a + 1)
                    pool.wait_ge(S.dotr_done, a + 1)
                    pool.tensor_tensor(part(5, 1), z_sb, kb_chan, ALU.mult).then_inc(S.p1_done, 1)
                if j == MAIN["y"]:
                    pool.wait_ge(S.ksd_done, a + 1)
                    pool.tensor_tensor(temp1, vb, temp2, ALU.subtract).then_inc(S.y_done, 1)
                if j == MAIN["o"]:
                    pool.wait_ge(S.u_done, a + 1)
                    pool.wait_ge(S.dotw_done, a + 1)
                    pool.tensor_tensor(temp2, temp2, qk_dot[:, :].unsqueeze(2).broadcast_to([P, NT, D]),
                                       ALU.mult).then_inc(S.uw_done, 1)
                if 0 <= j - MAIN["rms"] < NT:
                    i = NH * (j - MAIN["rms"])
                    pool.wait_ge(S.orms_done, a + 1)
                    pool.tensor_tensor(rms_r[:, i:i + NH], rms_ss[:, i:i + NH], minus_half[:, 0:NH],
                                       ALU.pow).then_inc(S.orr_done, 1)
                if j == MAIN["rstd"]:
                    pool.wait_ge(S.ve_done, a + 1)
                    pool.tensor_tensor(rstd[:, :], var_eps[:, :], minus_half[:, 0:NT], ALU.pow).then_inc(S.rstd_done, 1)

            def weighted(b, j):
                t, m = b * NJ + j, rows(j)
                if j < NS:
                    w = const[0:I, C_ONE:C_ONE + 1].broadcast_to([I, L])
                else:
                    pool.wait_ge(route_in[(j - NS) // TPG], 16 * (b + 1))
                    w = route_rows[:, (j - NS) // TPG, :]
                pool.wait_ge(S.m_done, t + 1)
                if some(t - 1):
                    pool.wait_ge(S.hlo_done, t - 1)
                pool.tensor_tensor(hid[0:m, j % 2, :], prod[0:m, j % 2, :], w, ALU.mult).then_inc(S.h_done, 1)

            def slot(j, b, n, ffn, main, pre, finish):
                if pre:
                    projections(b + 2, j)
                if main:
                    attention(b + 1, j)
                if finish and j == FINISH["rstd"]:
                    pool.wait_ge(S.ve2_done, b)
                    pool.tensor_tensor(rstd2[:, :], var_eps2[:, :], minus_half[:, 0:NT], ALU.pow).then_inc(S.rstd2_done, 1)
                if ffn:
                    weighted(b, j)

            pool.memset(minus_half[:, :], -0.5).then_inc(S.half_set, 1)
            pool.wait_ge(S.half_set, 1)
            pool.wait_ge(S.consts_in, 16)
            pool.wait_ge(S.taps_lo, KS)
            pool.wait_ge(S.small_lo, 1)
            for j in range(NJ):
                projections(0, j)
            walk(pool, slot)

        @block.scalar
        def _(act):
            def projections(c, j):
                if j == PRE["x_hi"]:
                    act.wait_ge(S.x_in0, 16 * (c + 1))
                    if some(c):
                        act.wait_ge(S.qkv_mm, NT * c)
                    act.activation(xc_hi[:, KS:KS + L], xc_raw[:, :], ACT.Copy).then_inc(S.xhi_done, 1)
                for i in range(NT):
                    if j == PRE["silu"][i]:
                        ps = (pa, pb)[i % 2]
                        act.wait_ge(S.qkv_mm, NT * c + i + 1)
                        if i == 0 and some(c):
                            act.wait_ge(S.osd_done, c)
                            act.wait_ge(S.t_done, c)
                        act.activation(qkv[:, i, :], ps[:, 0:QKV], ACT.Silu)
                        act.activation(tanh_b[:, i, :], ps[:, QKV:QKVB], ACT.Tanh, scale=0.5).then_inc(S.qkv_act, 1)
                        act.wait_ge(S.qkv_act, NT * c + i + 1)
                        act.activation(squares[:, i * 2 * D:(i + 1) * 2 * D], qkv[:, i, 0:2 * D],
                                       ACT.Square).then_inc(S.sq_done, 1)

            def attention(a, j, n):
                if j == MAIN["turn_k"]:
                    act.wait_ge(S.kt_mm, a + 1)
                    act.activation(k_chan, pa[:, :], ACT.Copy).then_inc(S.kt_done, 1)
                    if some(a):
                        act.wait_ge(S.rw_done, a)
                    act.activation(as_tiles(inv), eye, ACT.Copy).then_inc(S.eye_set, 1)
                if j == MAIN["turn_kb"]:
                    act.wait_ge(S.kbt_mm, a + 1)
                    act.activation(kb_chan, pb[:, :], ACT.Copy, scale=-1.0).then_inc(S.kbt_done, 1)
                    act.activation(as_tiles(inv_t), eye, ACT.Copy).then_inc(S.eye_t_set, 1)
                if j == MAIN["chunk_a"]:
                    act.wait_ge(S.at_mm, a + 1)
                    act.activation(neg_a_t, pa[:, :], ACT.Copy).then_inc(S.nat_done, 1)
                for k in range(1, LEVELS):
                    if j == MAIN["levels"] + 2 * (k - 1):
                        act.wait_ge(S.z_mm, (LEVELS - 1) * a + k)
                        act.activation(z_sb, pb[:, :], ACT.Copy).then_inc(S.z_done, 1)
                if j == MAIN["turn_v"]:
                    act.wait_ge(S.vt_mm, a + 1)
                    act.activation(vb_chan, pa[:, :], ACT.Copy).then_inc(S.vt_done, 1)
                if j == MAIN["scan"]:
                    act.wait_ge(S.state_done, a + 1)
                    act.activation(z_sb.rearrange("p (n c) -> p n c", c=C),
                                   state[:, 0:NC].unsqueeze(2).broadcast_to([P, NC, C]), ACT.Copy).then_inc(S.sx_done, 1)
                if j == MAIN["osq"]:
                    act.wait_ge(S.o_done, a + 1)
                    act.activation(temp1, o_sb, ACT.Square).then_inc(S.osq_done, 1)
                if j == MAIN["turn_o"]:
                    act.wait_ge(S.ont_mm, a + 1)
                    act.activation(on_chan, pc[:, :], ACT.Copy).then_inc(S.ont_done, 1)
                if j == MAIN["x1_turn"]:
                    act.wait_ge(S.x1t_mm, a + 1)
                    act.activation(x1_hi[n][:, :], pc[:, :], ACT.Copy).then_inc(S.x1hi_done, 1)
                if j == MAIN["logits"]:
                    act.wait_ge(S.logit_mm, a + 1)
                    act.activation(score, pc[:, 0:NT * E], ACT.Tanh, scale=0.5).then_inc(S.tanh_done, 1)
                if j == MAIN["route"]:
                    act.wait_ge(S.route_mm, a + 1)
                    if some(a):
                        act.wait_ge(route_in[RG - 1], 16 * a)
                    act.activation(expert_rows[:, :], pc[0:E, :], ACT.Copy).then_inc(S.route_done, 1)

            def silu_tile(b, j):
                t, m = b * NJ + j, rows(j)
                act.wait_ge(S.gate_mm, t + 1)
                if some(t - 1):
                    act.wait_ge(S.m_done, t - 1)
                act.activation(act_g[0:m, j % 2, :], gate_ps[j % 2][0:m, :], ACT.Silu).then_inc(S.s_done, 1)

            def hidden_hi(b, j, n):
                t, m, at = b * NJ + j, rows(j), place(j, n)
                act.wait_ge(S.h_done, t + 1)
                if some(t - HB + 1):
                    act.wait_ge(S.down_mm, t - HB + 1)
                act.activation(hid_hi[0:m, at, :], hid[0:m, j % 2, :], ACT.Copy).then_inc(S.hhi_done, 1)

            def chunk_high(c, m):
                n, at = c % 2, SHARED + c * CHUNK
                act.wait_ge(chunk_in[m][n], 16 * (c // 2 + 1))
                if m < 2:
                    act.activation((gate_hi, up_hi)[m][:, at:at + CHUNK], work[:, 2 * m + n, :], ACT.Copy).then_inc(S.chunk_hi, 1)
                else:
                    if c >= 2:
                        act.wait_ge(down_out[n], 16 * (c // 2))
                    act.activation(pairs(n)[:, :, 0, :].bitcast(F32R), work[:, 4 + n, :].rearrange("p (t c) -> p t c", c=P),
                                   ACT.Copy).then_inc(S.chunk_hi, 1)

            def slot(j, b, n, ffn, main, pre, finish):
                if finish and j == FINISH["y"]:
                    act.wait_ge(S.down_mm, NJ * b)
                    if some(b - 1):
                        act.wait_ge(S.out_done0, 16 * (b - 1))
                    act.activation(y_chan, y_ps[:, :], ACT.Copy).then_inc(S.yc_done, 1)
                if ffn:
                    silu_tile(b, j)
                if ffn and j >= 1:
                    hidden_hi(b, j - 1, n)
                if finish and j == 0:
                    hidden_hi(b - 1, NJ - 1, 1 - n)
                if main:
                    attention(b + 1, j, 1 - n)
                if pre:
                    projections(b + 2, j)
                if main and not ffn and j // 3 < NCHUNK:
                    chunk_high(j // 3, j % 3)

            act.dma_start(w_raw[:, QKV:QKVB], Wb).then_inc(S.conv_in, 16)
            for m, w in enumerate((Wq, Wk, Wv)):
                act.dma_start(w_raw[:, m * D:(m + 1) * D], w).then_inc(S.conv_in, 16)
            act.dma_start(const[:, :], consts).then_inc(S.consts_in, 16)
            act.wait_ge(S.half_set, 1)
            act.activation(rstd2[:, :], minus_half[:, 0:NT], ACT.Silu)
            at = 2 * SHARED + E
            projections(0, PRE["x_hi"])
            for k in reversed(range(KS)):
                act.wait_ge(S.tap_made, KS - k)
                act.activation(tap_hi[:, k, :], tap_raw[:, k, :], ACT.Copy).then_inc(S.taps_hi, 1)
            act.wait_ge(S.consts_in, 16)
            act.wait_ge(S.small_in, 16 * 9)
            act.activation(gate_hi[:, 0:SHARED], small_raw[:, 0:SHARED], ACT.Copy)
            act.activation(up_hi[:, 0:SHARED], small_raw[:, SHARED:2 * SHARED], ACT.Copy)
            act.activation(router_hi[:, :], small_raw[:, 2 * SHARED:2 * SHARED + E], ACT.Copy)
            act.activation(down_sh[0:I, :, 0, :], small_raw[0:I, at:at + NS * P]
                           .rearrange("p (s c) -> p s c", s=NS), ACT.Copy).then_inc(S.small_hi, 1)
            act.wait_ge(S.taps_lo, KS)
            for j in range(PRE["x_hi"] + 1, NJ):
                projections(0, j)
            walk(act, slot)

        @block.vector
        def _(dve):
            def projections(b, j):
                if j == PRE["x_lo"]:
                    dve.wait_ge(S.xhi_done, b + 1)
                    dve.tensor_tensor(xc_lo[:, KS:KS + L], xc_raw[:, :], xc_hi[:, KS:KS + L].bitcast(F32),
                                      ALU.subtract).then_inc(S.xlo_done, 1)
                for i in range(NT):
                    if j == PRE["sums"][i]:
                        dve.wait_ge(S.sq_done, NT * b + i + 1)
                        dve.tensor_reduce(head_ss[:, 8 * i:8 * i + 8], squares[:, i * 2 * D:(i + 1) * 2 * D]
                                          .rearrange("p (g d) -> p g d", d=HD), AX.X, ALU.add).then_inc(S.ss_done, 1)
                    if j == PRE["norm"][i]:
                        dve.wait_ge(S.rn_done, NT * b + i + 1)
                        qk = qkv[:, i, 0:2 * D].rearrange("p (g d) -> p g d", d=HD)
                        dve.tensor_tensor(qk, qk, head_rn[:, 8 * i:8 * i + 8].unsqueeze(2).broadcast_to([P, 2 * NH, HD]),
                                          ALU.mult).then_inc(S.qk_done, 1)
                if j == PRE["beta"]:
                    dve.wait_ge(S.qkv_act, NT * (b + 1))
                    dve.tensor_scalar(beta[:, :, :], tanh_b[:, :, :], 0.5, 0.5, ALU.mult, ALU.add).then_inc(S.beta_done, 1)

            def attention(b, j, n):
                if j == MAIN["chunk_a"]:
                    dve.wait_ge(S.zero_set, 1)
                    dve.wait_ge(S.a_mm, b + 1)
                    dve.wait_ge(S.eye_set, b + 1)
                    dve.copy_predicated(as_tiles(inv), mask_of(0, 0), as_tiles(pc[:, :])).then_inc(S.inv_done, 1)
                    dve.wait_ge(S.zero_set, 1)
                    dve.wait_ge(S.nat_done, b + 1)
                    dve.wait_ge(S.eye_t_set, b + 1)
                    dve.copy_predicated(as_tiles(inv_t), mask_of(0, 1), as_tiles(neg_a_t)).then_inc(S.invt_done, 1)
                if j == MAIN["levels"]:
                    dve.wait_ge(S.dot_done, b + 1)
                    dve.tensor_reduce(qk_dot[:, :], temp1, AX.X, ALU.add).then_inc(S.dotr_done, 1)
                    dve.wait_ge(S.dotr_done, b + 1)
                    dve.tensor_tensor(qk_dot[:, :], qk_dot[:, :], const[:, bass.ds(b + C_ROWS, 1)].broadcast_to([P, NT]),
                                      ALU.mult).then_inc(S.dotw_done, 1)
                for k in range(1, LEVELS):
                    if j == MAIN["levels"] + 2 * k - 1:
                        dve.wait_ge(S.zero_set, 1)
                        dve.wait_ge(inv_mm[k], b + 1)
                        dve.copy_predicated(as_tiles(inv), mask_of(k, 0), as_tiles(pc[:, :])).then_inc(S.inv_done, 1)
                        if k < LEVELS - 1:
                            dve.wait_ge(S.zero_set, 1)
                            dve.wait_ge(invt_mm[k], b + 1)
                            dve.copy_predicated(as_tiles(inv_t), mask_of(k, 1), as_tiles(pa[:, :])).then_inc(S.invt_done, 1)
                if j == MAIN["xk"]:
                    dve.wait_ge(S.xk_mm, b + 1)
                    dve.scalar_tensor_tensor(out=z_sb, in0=pb[:, :], scalar=1.5, in1=k_chan,
                                             op0=ALU.mult, op1=ALU.subtract).then_inc(S.g_done, 1)
                if j == MAIN["products"]:
                    dve.wait_ge(S.g_done, b + 1)
                    dve.wait_ge(S.vt_done, b + 1)
                    dve.tensor_tensor(part(6, 1), z_sb, vb_chan, ALU.mult).then_inc(S.p2_done, 1)
                if j == MAIN["sums"]:
                    dve.wait_ge(S.p1_done, b + 1)
                    dve.wait_ge(S.p2_done, b + 1)
                    dve.tensor_reduce(chunk_sums[:, :], part(5, 2).rearrange("p (n c) -> p n c", c=C), AX.X,
                                      ALU.add).then_inc(S.sums_done, 1)
                if j == MAIN["scan"]:
                    dve.wait_ge(S.sums_done, b + 1)
                    dve.tensor_scalar(decay[:, :], chunk_sums[:, 0:NC], 2.0, 1.0, ALU.mult, ALU.add)
                    dve.tensor_scalar(addition[:, :], chunk_sums[:, NC:2 * NC], 2.0, None, ALU.mult).then_inc(S.decay_done, 1)
                    dve.wait_ge(S.decay_done, b + 1)
                    dve.tensor_tensor_scan(state[:, 1:NC + 1], decay[:, :], addition[:, :], 0.0,
                                           ALU.mult, ALU.add).then_inc(S.state_done, 1)
                if j == MAIN["spread"]:
                    dve.wait_ge(S.sdb_mm, b + 1)
                    dve.tensor_tensor(temp2, kb, as_tiles(pa[:, :]), ALU.mult).then_inc(S.ksd_done, 1)
                    dve.tensor_tensor(o_sb, qkv[:, :, 0:D], as_tiles(pa[:, :]), ALU.mult).then_inc(S.osd_done, 1)
                if j == MAIN["tr"]:
                    dve.wait_ge(S.tr_mm, b + 1)
                    dve.scalar_tensor_tensor(out=temp2, in0=as_tiles(pb[:, :]), scalar=1.5,
                                             in1=temp1, op0=ALU.mult, op1=ALU.subtract).then_inc(S.u_done, 1)
                if j == MAIN["o"]:
                    dve.wait_ge(S.uw_done, b + 1)
                    dve.wait_ge(S.osd_done, b + 1)
                    dve.tensor_tensor(o_sb, o_sb, temp2, ALU.add).then_inc(S.o_done, 1)
                if j == MAIN["osq"]:
                    dve.wait_ge(S.osq_done, b + 1)
                    dve.tensor_reduce(rms_ss[:, :], temp1.rearrange("p i (h d) -> p (i h) d", d=HD), AX.X,
                                      ALU.add).then_inc(S.t_done, 1)
                    dve.wait_ge(S.t_done, b + 1)
                    dve.tensor_scalar(rms_ss[:, :], rms_ss[:, :], 1.0 / HD, RMS_EPS, ALU.mult,
                                      ALU.add).then_inc(S.orms_done, 1)
                if j == MAIN["on"]:
                    dve.wait_ge(S.orr_done, NT * (b + 1))
                    dve.tensor_tensor(on_sb.rearrange("p i (h d) -> p i h d", h=NH),
                                      o_sb.rearrange("p i (h d) -> p i h d", h=NH),
                                      rms_r[:, :].rearrange("p (i h) -> p i h", i=NT).unsqueeze(3)
                                      .broadcast_to([P, NT, NH, HD]), ALU.mult).then_inc(S.on_done, 1)
                if j == MAIN["wo"]:
                    dve.wait_ge(S.wo_mm, b + 1)
                    dve.wait_ge(S.x_in1, 16 * (b + 1))
                    dve.tensor_tensor(r1, as_tiles(pc[:, :]), x_res[:, :, :], ALU.add).then_inc(S.r1_done, 1)
                if j == MAIN["moments"]:
                    moments(b, r1, stats, mean_var, var_eps, S.r1_done,  S.st_done, S.mv_done, S.ve_done)
                if j == MAIN["x1"]:
                    dve.wait_ge(S.rstd_done, b + 1)
                    normalized(x1[n], r1, mean_var, rstd, S.x1_done)
                if j == MAIN["x1_lo"]:
                    dve.wait_ge(S.x1hi_done, b + 1)
                    dve.tensor_tensor(x1_lo[n][:, :], pc[:, :], x1_hi[n][:, :].bitcast(F32),
                                      ALU.subtract).then_inc(S.x1lo_done, 1)

            def moments(b, r, st, mv, ve, ready, st_sem, mv_sem, ve_sem):
                dve.wait_ge(ready, b + 1)
                for i in range(NT):
                    ins = dve.bn_stats(st[:, i, :], r[:, i, :])
                ins.then_inc(st_sem, 1)
                dve.wait_ge(S.zero_set, 1)
                dve.wait_ge(st_sem, b + 1)
                for i in range(NT):
                    ins = dve.bn_aggr(mv[:, i, :], st[:, i, :])
                ins.then_inc(mv_sem, 1)
                dve.wait_ge(mv_sem, b + 1)
                dve.tensor_scalar(ve[:, :], mv[:, :, 1], LN_EPS, None, ALU.add).then_inc(ve_sem, 1)

            def normalized(dst, r, mv, rs, done):
                for i in range(NT):
                    ins = dve.tensor_scalar(dst[:, i, :], r[:, i, :], mv[:, i, 0:1], rs[:, i:i + 1],
                                            ALU.subtract, ALU.mult)
                ins.then_inc(done, 1)

            def router(b, j):
                c8 = choice.rearrange("p (g e) -> p g e", e=EG)
                hi4, lo4 = tour1[:, 0:128].rearrange("p (g e) -> p g e", e=4), tour1[:, 128:256].rearrange("p (g e) -> p g e", e=4)
                hi2, mid2 = tour2[:, 0:64].rearrange("p (g e) -> p g e", e=2), tour2[:, 64:128].rearrange("p (g e) -> p g e", e=2)
                lo2 = tour2[:, 128:192].rearrange("p (g e) -> p g e", e=2)
                hi1, mid1, lo1 = (tour1[:, n:n + 32].unsqueeze(2) for n in (0, 32, 64))
                gs = group_sum[:, :].rearrange("p (i g) -> p i g", i=NT)
                other, own = gs.unsqueeze(2).broadcast_to([P, NT, NG, NG]), gs.unsqueeze(3).broadcast_to([P, NT, NG, NG])
                larger = tour1.rearrange("p (i g k) -> p i g k", i=NT, g=NG)
                equal = tour2.rearrange("p (i g k) -> p i g k", i=NT, g=NG)
                before = const[:, C_BEFORE:C_BEFORE + NG * NG].unsqueeze(1).broadcast_to([P, NT, NG * NG])
                if j == MAIN["router"] + 0:
                    dve.wait_ge(S.tanh_done, b + 1)
                    dve.tensor_scalar(score, score, 0.5, 0.5, ALU.mult, ALU.add).then_inc(S.score_done, 1)
                    dve.wait_ge(S.score_done, b + 1)
                    dve.tensor_tensor(choice.rearrange("p (i e) -> p i e", i=NT), score.rearrange("p (i e) -> p i e", i=NT),
                                      bias_b[:, :].unsqueeze(1).broadcast_to([P, NT, E]), ALU.add).then_inc(S.choice_done, 1)
                if j == MAIN["router"] + 1:
                    dve.wait_ge(S.choice_done, b + 1)
                    dve.tensor_tensor(hi4, c8[:, :, 0:4], c8[:, :, 4:8], ALU.max)
                    dve.tensor_tensor(lo4, c8[:, :, 0:4], c8[:, :, 4:8], ALU.min).then_inc(S.gs_done, 1)
                    dve.wait_ge(S.gs_done, 6 * b + 1)
                    dve.tensor_tensor(hi2, hi4[:, :, 0:2], hi4[:, :, 2:4], ALU.max)
                    dve.tensor_tensor(mid2, hi4[:, :, 0:2], hi4[:, :, 2:4], ALU.min)
                    dve.tensor_tensor(lo2, lo4[:, :, 0:2], lo4[:, :, 2:4], ALU.max).then_inc(S.gs_done, 1)
                if j == MAIN["router"] + 2:
                    dve.wait_ge(S.gs_done, 6 * b + 2)
                    dve.tensor_tensor(lo2, lo2, mid2, ALU.max).then_inc(S.gs_done, 1)
                    dve.wait_ge(S.gs_done, 6 * b + 3)
                    dve.tensor_tensor(hi1, hi2[:, :, 0:1], hi2[:, :, 1:2], ALU.max)
                    dve.tensor_tensor(mid1, hi2[:, :, 0:1], hi2[:, :, 1:2], ALU.min)
                    dve.tensor_tensor(lo1, lo2[:, :, 0:1], lo2[:, :, 1:2], ALU.max).then_inc(S.gs_done, 1)
                    dve.wait_ge(S.gs_done, 6 * b + 4)
                    dve.tensor_tensor(lo1, lo1, mid1, ALU.max).then_inc(S.gs_done, 1)
                    dve.wait_ge(S.gs_done, 6 * b + 5)
                    dve.tensor_tensor(group_sum[:, :].unsqueeze(2), hi1, lo1, ALU.add).then_inc(S.gs_done, 1)
                if j == MAIN["router"] + 3:
                    dve.wait_ge(S.gs_done, 6 * b + 6)
                    dve.tensor_tensor(larger, other, own, ALU.is_gt)
                    dve.tensor_tensor(equal, other, own, ALU.is_equal).then_inc(S.gt_done, 1)
                    dve.wait_ge(S.gt_done, 3 * b + 1)
                    dve.tensor_tensor(tour2.rearrange("p (i k) -> p i k", i=NT), tour2.rearrange("p (i k) -> p i k", i=NT),
                                      before, ALU.mult).then_inc(S.gt_done, 1)
                    dve.wait_ge(S.gt_done, 3 * b + 2)
                    dve.tensor_tensor(tour1, tour1, tour2, ALU.add).then_inc(S.gt_done, 1)
                if j == MAIN["router"] + 4:
                    dve.wait_ge(S.gt_done, 3 * b + 3)
                    dve.tensor_reduce(group_rank[:, :], tour1.rearrange("p (g k) -> p g k", k=NG), AX.X, ALU.add).then_inc(S.rank_done, 1)
                    dve.wait_ge(S.rank_done, b + 1)
                    dve.tensor_scalar(group_on[:, :], group_rank[:, :], GROUPS_KEPT - 0.5, None, ALU.is_lt).then_inc(S.gon_done, 1)
                if j == MAIN["router"] + 5:
                    dve.wait_ge(S.gon_done, b + 1)
                    dve.tensor_tensor(masked.rearrange("p (g e) -> p g e", e=EG), c8,
                                      group_on[:, :].unsqueeze(2).broadcast_to([P, NT * NG, EG]), ALU.mult).then_inc(S.mask_done, 1)
                    dve.wait_ge(S.mask_done, b + 1)
                    dve.tensor_scalar(masked, masked, 0.0, None, ALU.add).then_inc(S.masked_done, 1)
                if j == MAIN["router"] + 6:
                    dve.wait_ge(S.zero_set, 1)
                    dve.wait_ge(S.masked_done, b + 1)
                    for i in range(NT):
                        ins = dve.max(top8[:, i, :], masked[:, i * E:(i + 1) * E])
                    ins.then_inc(S.top_done, 1)
                    dve.wait_ge(S.zero_set, 1)
                    dve.wait_ge(S.top_done, b + 1)
                    for i in range(NT):
                        ins = dve.match_replace(replaced[:, i * E:(i + 1) * E], top8[:, i, :], masked[:, i * E:(i + 1) * E], TAKEN)
                    ins.then_inc(S.rep_done, 1)
                if j == MAIN["router"] + 7:
                    dve.wait_ge(S.rep_done, b + 1)
                    dve.scalar_tensor_tensor(out=tour1, in0=replaced, scalar=TAKEN, in1=score, op0=ALU.is_equal,
                                             op1=ALU.mult).then_inc(S.w_done, 1)
                    dve.wait_ge(S.w_done, b + 1)
                    dve.tensor_reduce(weight_sum[:, :], tour1.rearrange("p (i e) -> p i e", i=NT), AX.X, ALU.add).then_inc(S.ws_done, 1)
                    dve.wait_ge(S.ws_done, 2 * b + 1)
                    dve.tensor_scalar(weight_sum[:, :], weight_sum[:, :], 1e-20, None, ALU.add).then_inc(S.ws_done, 1)
                    dve.wait_ge(S.ws_done, 2 * b + 2)
                    dve.reciprocal(weight_inv[:, :], weight_sum[:, :]).then_inc(S.wi_done, 1)
                    dve.wait_ge(S.wi_done, b + 1)
                    dve.scalar_tensor_tensor(out=routing[:, :, :], in0=tour1.rearrange("p (i e) -> p i e", i=NT),
                                             scalar=ROUTED_SCALE, in1=weight_inv[:, :].unsqueeze(2).broadcast_to([P, NT, E]),
                                             op0=ALU.mult, op1=ALU.mult).then_inc(S.rw_done, 1)

            def product_tile(b, j):
                t, m = b * NJ + j, rows(j)
                dve.wait_ge(S.s_done, t + 1)
                dve.wait_ge(S.up_mm, t + 1)
                if some(t - 1):
                    dve.wait_ge(S.h_done, t - 1)
                dve.tensor_tensor(prod[0:m, j % 2, :], up_ps[j % 2][0:m, :], act_g[0:m, j % 2, :],
                                  ALU.mult).then_inc(S.m_done, 1)

            def hidden_lo(b, j, n):
                t, m, at = b * NJ + j, rows(j), place(j, n)
                dve.wait_ge(S.hhi_done, t + 1)
                if some(t - HB + 1):
                    dve.wait_ge(S.down_mm, t - HB + 1)
                dve.tensor_tensor(hid_lo[0:m, at, :], hid[0:m, j % 2, :], hid_hi[0:m, at, :].bitcast(F32),
                                  ALU.subtract).then_inc(S.hlo_done, 1)

            def last_norm(b, j, n):
                if j == FINISH["y"]:
                    dve.wait_ge(S.yt_mm, b + 1)
                    dve.tensor_tensor(r2[:, :, :], as_tiles(y_ps[:, :]), x1[n][:, :, :], ALU.add).then_inc(S.r2_done, 1)
                if j == FINISH["moments"]:
                    moments(b, r2, stats2, mean_var2, var_eps2, S.r2_done, S.st2_done, S.mv2_done, S.ve2_done)
                if j == FINISH["norm"]:
                    dve.wait_ge(S.rstd2_done, b + 1)
                    normalized(r2, r2, mean_var2, rstd2, S.ln2_done)

            def chunk_low(c, m):
                n, at = c % 2, SHARED + c * CHUNK
                dve.wait_ge(S.chunk_hi, 3 * c + m + 1)
                if m < 2:
                    hi, lo = ((gate_hi, gate_lo), (up_hi, up_lo))[m]
                    dve.tensor_tensor(lo[:, at:at + CHUNK], work[:, 2 * m + n, :], hi[:, at:at + CHUNK].bitcast(F32),
                                      ALU.subtract).then_inc(S.chunk_lo, 1)
                else:
                    dve.tensor_tensor(pairs(n)[:, :, 1, :].bitcast(F32R), work[:, 4 + n, :].rearrange("p (t c) -> p t c", c=P),
                                      pairs(n)[:, :, 0, :], ALU.subtract).then_inc(S.chunk_lo, 1)

            def slot(j, b, n, ffn, main, pre, finish):
                if finish and j == FINISH["y"]:
                    last_norm(b - 1, j, 1 - n)
                if ffn:
                    product_tile(b, j)
                if ffn and j >= 1:
                    hidden_lo(b, j - 1, n)
                if finish and j == 0:
                    hidden_lo(b - 1, NJ - 1, 1 - n)
                if finish and j > FINISH["y"]:
                    last_norm(b - 1, j, 1 - n)
                if main:
                    attention(b + 1, j, 1 - n)
                    router(b + 1, j)
                if pre:
                    projections(b + 2, j)
                if main and not ffn and j // 3 < NCHUNK:
                    chunk_low(j // 3, j % 3)

            dve.memset(xc_hi[:, 0:KS].bitcast(F32), 0.0)
            dve.memset(xc_lo[:, 0:KS].bitcast(F32), 0.0)
            dve.memset(state[:, 0:1], 0.0).then_inc(S.zero_set, 1)
            dve.wait_ge(S.conv_in, 16 * 7)
            for k in reversed(range(KS)):
                dve.tensor_tensor(tap_raw[:, k, 0:QKV], w_raw[:, 0:QKV],
                                  conv_b.rearrange("p (n k) -> p n k", k=KS)[:, :, k], ALU.mult)
                dve.tensor_copy(tap_raw[:, k, QKV:QKVB], w_raw[:, QKV:QKVB]).then_inc(S.tap_made, 1)
            for k in reversed(range(KS)):
                dve.wait_ge(S.taps_hi, KS - k)
                dve.tensor_tensor(tap_lo[:, k, :], tap_raw[:, k, :], tap_hi[:, k, :].bitcast(F32),
                                  ALU.subtract).then_inc(S.taps_lo, 1)
                if k == KS - 1:
                    projections(0, PRE["x_lo"])
            dve.wait_ge(S.small_in, 16 * 9)
            at = 2 * SHARED + E + NS * P
            dve.tensor_scalar(wo_g[:, :], small_raw[:, at:at + D], g_col[:, 0:1], None, ALU.mult).then_inc(S.wo_made, 1)
            dve.wait_ge(S.small_hi, 1)
            dve.tensor_tensor(gate_lo[:, 0:SHARED], small_raw[:, 0:SHARED], gate_hi[:, 0:SHARED].bitcast(F32), ALU.subtract)
            dve.tensor_tensor(up_lo[:, 0:SHARED], small_raw[:, SHARED:2 * SHARED], up_hi[:, 0:SHARED].bitcast(F32), ALU.subtract)
            dve.tensor_tensor(router_lo[:, :], small_raw[:, 2 * SHARED:2 * SHARED + E], router_hi[:, :].bitcast(F32), ALU.subtract)
            dve.tensor_tensor(down_sh[0:I, :, 1, :], small_raw[0:I, 2 * SHARED + E:at].rearrange("p (s c) -> p s c", s=NS),
                              down_sh[0:I, :, 0, :].bitcast(F32), ALU.subtract).then_inc(S.small_lo, 1)

            dve.wait_ge(S.masks_in, 16 * 2)
            for j in range(PRE["x_lo"] + 1, NJ):
                projections(0, j)
            walk(dve, slot)

        @block.tensor
        def _(pe):
            def three(ps, lhs, rhs, start=True, stop=True):
                pe.matmul(ps, lhs[0], rhs[0], start=start, stop=False)
                pe.matmul(ps, lhs[0], rhs[1], start=False, stop=False)
                return pe.matmul(ps, lhs[1], rhs[0], start=False, stop=stop)

            def tiles(ps, lhs, rhs):
                for i in range(NT):
                    mm = pe.matmul(blk(ps, i), lhs(i), rhs(i), start=True, stop=True)
                return mm

            def turned(ps, src):
                for i in range(NT):
                    mm = pe.transpose(blk(ps, i), src(i), ident)
                return mm

            def projections(c, j):
                for i in range(NT):
                    half = j - PRE["conv"][i]
                    if half not in (0, 1):
                        continue
                    ps = (pa, pb)[i % 2]
                    pe.wait_ge(S.xlo_done, c + 1)
                    if half == 0 and i < 2 and some(c):
                        pe.wait_ge((S.osd_done, S.u_done)[i], c)
                    if half == 0 and i >= 2:
                        pe.wait_ge(S.qkv_act, NT * c + i - 1)
                    for k in ((3, 2), (1, 0))[half]:
                        if i == 0 and not some(c):
                            pe.wait_ge(S.taps_lo, KS - k)
                        m = QKVB if k == KS - 1 else QKV
                        at = i * P + k + 1
                        mm = three(ps[:, 0:m], (xc_hi[:, at:at + P], xc_lo[:, at:at + P]),
                                   (tap_hi[:, k, 0:m], tap_lo[:, k, 0:m]), start=(k == KS - 1), stop=(k == 0))
                    if half == 1:
                        mm.then_inc(S.qkv_mm, 1)

            def attention(a, j, n):
                if j == MAIN["turn_k"]:
                    pe.wait_ge(S.qk_done, NT * (a + 1))
                    turned(pa, lambda i: qkv[:, i, D:2 * D]).then_inc(S.kt_mm, 1)
                if j == MAIN["turn_kb"]:
                    pe.wait_ge(S.kb_done, a + 1)
                    turned(pb, lambda i: kb[:, i, :]).then_inc(S.kbt_mm, 1)
                if j == MAIN["chunk_a"]:
                    pe.wait_ge(S.kt_done, a + 1)
                    pe.wait_ge(S.kbt_done, a + 1)
                    if some(a):
                        pe.wait_ge(S.route_done, a)
                    tiles(pc, lambda i: blk(kb_chan, i), lambda i: blk(k_chan, i)).then_inc(S.a_mm, 1)
                    tiles(pa, lambda i: blk(k_chan, i), lambda i: blk(kb_chan, i)).then_inc(S.at_mm, 1)
                for k in range(1, LEVELS):
                    if j == MAIN["levels"] + 2 * (k - 1):
                        pe.wait_ge(S.nat_done, a + 1)
                        pe.wait_ge(S.inv_done, LEVELS * a + k)
                        tiles(pb, lambda i: blk(neg_a_t, i), lambda i: blk(inv, i)).then_inc(S.z_mm, 1)
                    if j == MAIN["levels"] + 2 * k - 1:
                        pe.wait_ge(S.z_done, (LEVELS - 1) * a + k)
                        pe.wait_ge(S.invt_done, (LEVELS - 1) * a + k)
                        tiles(pc, lambda i: blk(inv_t, i), lambda i: blk(z_sb, i)).then_inc(inv_mm[k], 1)
                        if k < LEVELS - 1:
                            tiles(pa, lambda i: blk(z_sb, i), lambda i: blk(inv_t, i)).then_inc(invt_mm[k], 1)
                if j == MAIN["turn_v"]:
                    pe.wait_ge(S.vb_done, a + 1)
                    pe.wait_ge(S.invt_done, (LEVELS - 1) * (a + 1))
                    turned(pa, lambda i: vb[:, i, :]).then_inc(S.vt_mm, 1)
                if j == MAIN["xk"]:
                    pe.wait_ge(S.inv_done, LEVELS * (a + 1))
                    tiles(pb, lambda i: qkv[:, i, D:2 * D], lambda i: blk(inv, i)).then_inc(S.xk_mm, 1)
                if j == MAIN["spread"]:
                    pe.wait_ge(S.sx_done, a + 1)
                    turned(pa, lambda i: blk(z_sb, i)).then_inc(S.sdb_mm, 1)
                if j == MAIN["tr"]:
                    pe.wait_ge(S.y_done, a + 1)
                    tiles(pb, lambda i: blk(inv_t, i), lambda i: temp1[:, i, :]).then_inc(S.tr_mm, 1)
                if j == MAIN["turn_o"]:
                    pe.wait_ge(S.on_done, a + 1)
                    turned(pc, lambda i: on_sb[:, i, :]).then_inc(S.ont_mm, 1)
                if j == MAIN["wo"]:
                    pe.wait_ge(S.ont_done, a + 1)
                    tiles(pc, lambda i: blk(on_chan, i), lambda i: wo_g[:, :]).then_inc(S.wo_mm, 1)
                if j == MAIN["x1_turn"]:
                    pe.wait_ge(S.x1_done, a + 1)
                    turned(pc, lambda i: x1[n][:, i, :]).then_inc(S.x1t_mm, 1)
                if j == MAIN["logits"]:
                    pe.wait_ge(S.x1lo_done, a + 1)
                    for i in range(NT):
                        mm = three(pc[:, i * E:(i + 1) * E], (blk(x1_hi[n], i), blk(x1_lo[n], i)),
                                   (router_hi[:, :], router_lo[:, :]))
                    mm.then_inc(S.logit_mm, 1)
                if j == MAIN["route"]:
                    pe.wait_ge(S.zero_set, 1)
                    pe.wait_ge(S.rw_done, a + 1)
                    for i in range(NT):
                        mm = pe.transpose(pc[0:E, i * P:(i + 1) * P], routing[:, i, :], ident)
                    mm.then_inc(S.route_mm, 1)

            def gate_up(b, j, n):
                lo, hi = cols(j)
                t, m = b * NJ + j, rows(j)
                x = (x1_hi[n][:, :], x1_lo[n][:, :])
                if j == 0:
                    pe.wait_ge(S.x1lo_done, b + 1)
                if some(t - 1):
                    pe.wait_ge(S.s_done, t - 1)
                three(gate_ps[j % 2][0:m, :], (gate_hi[:, lo:hi], gate_lo[:, lo:hi]), x).then_inc(S.gate_mm, 1)
                if some(t - 1):
                    pe.wait_ge(S.m_done, t - 1)
                three(up_ps[j % 2][0:m, :], (up_hi[:, lo:hi], up_lo[:, lo:hi]), x).then_inc(S.up_mm, 1)

            def down(b, j, n):
                t, m, at = b * NJ + j, rows(j), place(j, n)
                if j >= NS:
                    k = (j - NS) % RING
                    pe.wait_ge(ring_in[k], 16 * (b * (NR // RING) + (j - NS) // RING + 1))
                    w = down_ring[:, k, 0, :], down_ring[:, k, 1, :]
                else:
                    w = down_sh[0:m, j, 0, :], down_sh[0:m, j, 1, :]
                pe.wait_ge(S.hlo_done, t + 1)
                if j == 0 and some(b):
                    pe.wait_ge(S.r2_done, b)
                three(y_ps[:, :], w, (hid_hi[0:m, at, :], hid_lo[0:m, at, :]), start=(j == 0),
                      stop=(j == NJ - 1)).then_inc(S.down_mm, 1)

            def slot(j, b, n, ffn, main, pre, finish):
                if ffn and not finish and j == 0:
                    pe.wait_ge(S.chunk_lo, 3 * NCHUNK)
                    pe.wait_ge(S.small_lo, 1)
                if ffn:
                    gate_up(b, j, n)
                if finish and j == FINISH["y"]:
                    pe.wait_ge(S.yc_done, b)
                    turned(y_ps, lambda i: blk(y_chan, i)).then_inc(S.yt_mm, 1)
                if main:
                    attention(b + 1, j, 1 - n)
                if pre:
                    projections(b + 2, j)
                if ffn and j >= LAG:
                    down(b, j - LAG, n)
                if finish and j < LAG:
                    down(b - 1, NJ - LAG + j, 1 - n)

            pe.wait_ge(S.consts_in, 16)
            pe.wait_ge(S.zero_set, 1)
            for j in range(NJ):
                projections(0, j)
            pe.wait_ge(S.wo_made, 1)
            pe.wait_ge(S.small_lo, 1)
            walk(pe, slot)


def kernel(**inputs):
    import numpy as np
    import concourse.bacc as bacc
    from concourse.bass_utils import run_bass_kernel_spmd

    def laid(name):
        return np.ascontiguousarray(inputs[name])

    x = laid("L0_attn_x")
    by_tile = lambda w: np.ascontiguousarray(
        w.reshape(RG, EP, TPG, ER, D).transpose(4, 0, 2, 1, 3).reshape(D, NR * P))
    wd = laid("L0_ffn_Wd").reshape(RG, EP, D, TPG, ER).transpose(1, 4, 0, 3, 2).reshape(P, NR * P)
    sd = laid("L0_ffn_Sd").T.reshape(NS, I, D).transpose(1, 0, 2).reshape(I, NS * D)

    consts = np.zeros((P, C_ALL), np.float32)
    t = np.arange(P)
    consts[:, C_ID:C_ID + P] = np.eye(P)
    consts[:, C_ROWS:C_ROWS + B] = 2.0 * (t[:, None] % C <= np.arange(B)[None, :])
    consts[:, C_BEFORE:C_BEFORE + NG * NG] = np.tril(np.ones((NG, NG)), -1).reshape(1, -1)
    consts[:, C_ONE] = 1.0
    masks = np.zeros((P, 2 * LEVELS, P), np.float32)
    for k in range(LEVELS):
        n = 1 << k
        low = (t[:, None] // (2 * n) == t[None, :] // (2 * n)) & (t[:, None] // n % 2 == 1) & (t[None, :] // n % 2 == 0)
        masks[:, 2 * k] = low
        masks[:, 2 * k + 1] = low.T

    arrays = {
        "x_tok": x, "x_chan": np.ascontiguousarray(x.reshape(B * L, D).T),
        "Wq": laid("L0_attn_Wq"), "Wk": laid("L0_attn_Wk"), "Wv": laid("L0_attn_Wv"), "Wb": laid("L0_attn_Wb"),
        "conv_q": laid("L0_attn_conv_q"), "conv_k": laid("L0_attn_conv_k"), "conv_v": laid("L0_attn_conv_v"),
        "g_rms": laid("L0_attn_g"), "Wo": laid("L0_attn_Wo"),
        "gate_wT": np.ascontiguousarray(laid("L0_ffn_gate_w").T), "gate_bias": laid("L0_ffn_gate_bias"),
        "gateT": by_tile(laid("L0_ffn_Wg")), "upT": by_tile(laid("L0_ffn_Wu")), "downT": np.ascontiguousarray(wd),
        "shared_gateT": np.ascontiguousarray(laid("L0_ffn_Sg").T), "shared_upT": np.ascontiguousarray(laid("L0_ffn_Su").T),
        "shared_downT": np.ascontiguousarray(sd), "consts": consts, "masks": masks,
    }
    nc = bacc.Bacc("TRN2", target_bir_lowering=False, num_devices=1)
    args = [nc.dram_tensor(n, a.shape, mybir.dt.from_np(a.dtype), kind="ExternalInput").ap() for n, a in arrays.items()]
    args.append(nc.dram_tensor("out", (B, L, D), F32, kind="ExternalOutput").ap())
    block_program(nc, *args)
    r = run_bass_kernel_spmd(nc, [arrays], core_ids=[0])
    return r.results[0]["out"]
```
